# Optimizing a Trainium2 kernel written in Bass

```python
import numpy as np
import jax
import jax.numpy as jnp

def _softmax(x, axis=-1):
    return jax.nn.softmax(x, axis=axis)

def _gelu(x):
    return jax.nn.gelu(x, approximate=True)

def _silu(x):
    return jax.nn.silu(x)

def _sigmoid(x):
    return jax.nn.sigmoid(x)

def _layernorm(x, axis=-1, eps=1e-05):
    m = jnp.mean(x, axis=axis, keepdims=True)
    v = jnp.var(x, axis=axis, keepdims=True)
    return (x - m) / jnp.sqrt(v + eps)

def _scatter_add(tgt, idx, src, axis=0):
    return tgt.at[idx].add(src)

def _segment_sum(src, seg, n):
    return jax.ops.segment_sum(src, seg, n)
kernel_name = 'mk_decoder_postln_d1_seqx_r2_e0f250'

def setup_inputs(seed: int=0):
    np.random.seed(seed)
    _w = jnp.asarray

    def _rec_inputs():
        import jax
        import jax.numpy as jnp
        _rk = jax.random.key(seed)
        x = -0.0002928 + 1 * jax.random.normal(jax.random.fold_in(_rk, 1), (8, 512, 512), jnp.float32)
        _lenS = 512 - jax.random.randint(jax.random.fold_in(_rk, 7), (8,), 0, max(1, 512 // 4) + 1, jnp.int32)
        _lenS2 = 512 - jax.random.randint(jax.random.fold_in(_rk, 8), (8,), 0, max(1, 512 // 4) + 1, jnp.int32)
        _ctx_1024P = jax.random.normal(jax.random.fold_in(_rk, 11), (8, 16, 512), jnp.float32)
        _ctx_1024c = jax.random.dirichlet(jax.random.fold_in(_rk, 511), 0.3 * jnp.ones((16,), jnp.float32), (8, 512))
        _ctx_1024t = jnp.einsum('bsk,bkd->bsd', _ctx_1024c, _ctx_1024P)
        _ctx_1024t = _ctx_1024t * jax.lax.rsqrt(jnp.mean(jnp.square(_ctx_1024t)) + 1e-12) * 0.953939
        ctx_1024 = -1.39393e-06 + 0.999914 * (_ctx_1024t + 0.3 * jax.random.normal(jax.random.fold_in(_rk, 611), (8, 512, 512), jnp.float32))
        return (x, ctx_1024)
    x, ctx_1024 = _rec_inputs()

    def _L0_attn_setup():
        import jax, jax.numpy as jnp
        import numpy as np
        from jax import lax
        D_MODEL = 512
        KERNEL = 5
        PAD = (KERNEL - 1) // 2
        key = jax.random.key(seed)
        k1, k2, k3, k4, k5 = jax.random.split(key, 5)
        B, T, D = (8, 2048, D_MODEL)
        x = jax.random.normal(k1, (B, T, D), dtype=jnp.float32)
        decay_logit = jnp.zeros((D,), dtype=jnp.float32)
        lim = 1.0 / np.sqrt(D)
        W = jax.random.uniform(k2, (D, D), minval=-lim, maxval=lim, dtype=jnp.float32)
        b = jax.random.uniform(k3, (D,), minval=-lim, maxval=lim, dtype=jnp.float32)
        limc = 1.0 / np.sqrt(KERNEL)
        conv_w = jax.random.uniform(k4, (D, 1, KERNEL), minval=-limc, maxval=limc, dtype=jnp.float32)
        conv_b = jax.random.uniform(k5, (D,), minval=-limc, maxval=limc, dtype=jnp.float32)
        return {'x': x, 'decay_logit': decay_logit, 'W': W, 'b': b, 'conv_w': conv_w, 'conv_b': conv_b}
    _L0_attn_all = _L0_attn_setup()
    _L0_attn_in = {k: v for k, v in _L0_attn_all.items() if k in ('decay_logit', 'W', 'b', 'conv_w', 'conv_b')}
    del _L0_attn_all

    def _L0_xattn_setup():
        import jax, jax.numpy as jnp
        import numpy as np
        B, S, D, NH = (2, 1024, 512, 8)
        DH = D // NH
        EPS = 1e-06
        LN_EPS = 1e-05

        def _mlstm_cell(q, k, v, igate_w, igate_b, fgate_w, fgate_b, ln_scale):
            Slen = q.shape[0]
            ifg = jnp.concatenate([q, k, v], axis=-1)
            ig = (ifg @ igate_w.T + igate_b).T
            fg = (ifg @ fgate_w.T + fgate_b).T
            qh = q.reshape(Slen, NH, DH).transpose(1, 0, 2)
            kh = k.reshape(Slen, NH, DH).transpose(1, 0, 2)
            vh = v.reshape(Slen, NH, DH).transpose(1, 0, 2)
            log_f = jax.nn.log_sigmoid(fg)
            cs = jnp.cumsum(log_f, axis=1)
            fg_mat = cs[:, :, None] - cs[:, None, :]
            mask = jnp.tril(jnp.ones((Slen, Slen), dtype=bool))
            log_fg_mat = jnp.where(mask, fg_mat, -jnp.inf)
            log_D = log_fg_mat + ig[:, None, :]
            max_log_D = jnp.max(log_D, axis=-1, keepdims=True)
            D_mat = jnp.exp(log_D - max_log_D)
            qk = jnp.einsum('hsd,htd->hst', qh, kh) / np.sqrt(DH)
            C = qk * D_mat
            normalizer = jnp.maximum(jnp.abs(C.sum(axis=-1, keepdims=True)), jnp.exp(-max_log_D))
            h = jnp.einsum('hst,htd->hsd', C / (normalizer + EPS), vh)
            h = h.transpose(1, 0, 2).reshape(Slen, D)
            mu = h.mean(axis=-1, keepdims=True)
            var = h.var(axis=-1, keepdims=True)
            return (h - mu) / jnp.sqrt(var + LN_EPS) * ln_scale
        key = jax.random.key(seed)
        ks = jax.random.split(key, 8)
        rnd = lambda k, sh, s=1.0: jax.random.normal(k, sh, dtype=jnp.float32) * s
        return {'q': rnd(ks[0], (B, S, D)), 'k': rnd(ks[1], (B, S, D)), 'v': rnd(ks[2], (B, S, D)), 'igate_w': rnd(ks[3], (NH, 3 * D), 0.02), 'igate_b': jnp.linspace(3.0, 6.0, NH, dtype=jnp.float32), 'fgate_w': rnd(ks[4], (NH, 3 * D), 0.02), 'fgate_b': rnd(ks[5], (NH,), 0.3162278), 'ln_scale': jnp.ones((D,), dtype=jnp.float32)}
    _L0_xattn_all = _L0_xattn_setup()
    _L0_xattn_in = {k: v for k, v in _L0_xattn_all.items() if k in ('igate_w', 'igate_b', 'fgate_w', 'fgate_b', 'ln_scale')}
    del _L0_xattn_all

    def _L0_ffn_setup():
        import jax, jax.numpy as jnp
        import numpy as np
        E, G, TOPK = (32, 16, 2)
        HID, INTER, A_INTER = (512, 1024, 128)
        CAP_FACTOR = 1.25
        SCALE = 0.05

        def _stats(x):
            mean = x.mean(-1, keepdims=True)
            std = jnp.std(x, axis=-1, keepdims=True, ddof=1)
            mn = x.min(-1, keepdims=True)
            mx = x.max(-1, keepdims=True)
            l2 = jnp.linalg.norm(x, axis=-1, keepdims=True)
            sp = (jnp.abs(x) < 1e-06).astype(x.dtype).mean(-1, keepdims=True)
            return jnp.concatenate([mean, std, mn, mx, l2, sp], -1)
        key = jax.random.key(seed)
        ks = jax.random.split(key, 8)
        B, N = (4, 512)
        s = lambda k, shape, sc: jax.random.normal(k, shape, jnp.float32) * sc
        return {'x': jax.random.normal(ks[0], (B, N, HID), jnp.float32), 'r1_w': s(ks[1], (HID // 2, HID + 6), 0.02), 'r1_b': jnp.zeros((HID // 2,), jnp.float32), 'r2_w': s(ks[2], (E, HID // 2), 0.02), 'w_up': s(ks[3], (E, 2 * INTER, HID), 0.02), 'w_down': s(ks[4], (E, HID, INTER), 0.02), 'a_up': s(ks[5], (G, 2 * A_INTER, HID), 0.02), 'a_down': s(ks[6], (G, HID, A_INTER), 0.02)}
    _L0_ffn_all = _L0_ffn_setup()
    _L0_ffn_in = {k: v for k, v in _L0_ffn_all.items() if k in ('r1_w', 'r1_b', 'r2_w', 'w_up', 'w_down', 'a_up', 'a_down')}
    del _L0_ffn_all
    return {'x': x, 'ctx_1024': ctx_1024, 'L0_attn_decay_logit': _L0_attn_in['decay_logit'], 'L0_attn_W': _L0_attn_in['W'], 'L0_attn_b': _L0_attn_in['b'], 'L0_attn_conv_w': _L0_attn_in['conv_w'], 'L0_attn_conv_b': _L0_attn_in['conv_b'], 'L0_xattn_igate_w': _L0_xattn_in['igate_w'], 'L0_xattn_igate_b': _L0_xattn_in['igate_b'], 'L0_xattn_fgate_w': _L0_xattn_in['fgate_w'], 'L0_xattn_fgate_b': _L0_xattn_in['fgate_b'], 'L0_xattn_ln_scale': _L0_xattn_in['ln_scale'], 'L0_ffn_r1_w': _L0_ffn_in['r1_w'], 'L0_ffn_r1_b': _L0_ffn_in['r1_b'], 'L0_ffn_r2_w': _L0_ffn_in['r2_w'], 'L0_ffn_w_up': _L0_ffn_in['w_up'], 'L0_ffn_w_down': _L0_ffn_in['w_down'], 'L0_ffn_a_up': _L0_ffn_in['a_up'], 'L0_ffn_a_down': _L0_ffn_in['a_down']}

def reference(x, ctx_1024, L0_attn_decay_logit, L0_attn_W, L0_attn_b, L0_attn_conv_w, L0_attn_conv_b, L0_xattn_igate_w, L0_xattn_igate_b, L0_xattn_fgate_w, L0_xattn_fgate_b, L0_xattn_ln_scale, L0_ffn_r1_w, L0_ffn_r1_b, L0_ffn_r2_w, L0_ffn_w_up, L0_ffn_w_down, L0_ffn_a_up, L0_ffn_a_down):
    import jax
    import jax.numpy as jnp

    def _L0_attn_ref(x, decay_logit, W, b, conv_w, conv_b):
        import jax, jax.numpy as jnp
        import numpy as np
        from jax import lax
        D_MODEL = 512
        KERNEL = 5
        PAD = (KERNEL - 1) // 2
        B, T, D = x.shape
        a = jax.nn.sigmoid(decay_logit)

        def step(s, xt):
            s = a * s + (1.0 - a) * xt
            return (s, s)
        s0 = jnp.zeros((B, D), dtype=x.dtype)
        _, S = lax.scan(step, s0, jnp.swapaxes(x, 0, 1))
        y_ret = jnp.einsum('tbd,ed->tbe', S, W) + b
        y_ret = jnp.swapaxes(y_ret, 0, 1)
        xc = jnp.swapaxes(x, 1, 2)
        y_loc = lax.conv_general_dilated(xc, conv_w, window_strides=(1,), padding=[(PAD, PAD)], feature_group_count=D)
        y_loc = y_loc + conv_b[None, :, None]
        y_loc = jnp.swapaxes(y_loc, 1, 2)
        return y_ret + y_loc

    def _L0_xattn_ref(q, k, v, igate_w, igate_b, fgate_w, fgate_b, ln_scale):
        import jax, jax.numpy as jnp
        import numpy as np
        B, S, D, NH = (2, 1024, 512, 8)
        DH = D // NH
        EPS = 1e-06
        LN_EPS = 1e-05

        def _mlstm_cell(q, k, v, igate_w, igate_b, fgate_w, fgate_b, ln_scale):
            Slen = q.shape[0]
            ifg = jnp.concatenate([q, k, v], axis=-1)
            ig = (ifg @ igate_w.T + igate_b).T
            fg = (ifg @ fgate_w.T + fgate_b).T
            qh = q.reshape(Slen, NH, DH).transpose(1, 0, 2)
            kh = k.reshape(Slen, NH, DH).transpose(1, 0, 2)
            vh = v.reshape(Slen, NH, DH).transpose(1, 0, 2)
            log_f = jax.nn.log_sigmoid(fg)
            cs = jnp.cumsum(log_f, axis=1)
            fg_mat = cs[:, :, None] - cs[:, None, :]
            mask = jnp.tril(jnp.ones((Slen, Slen), dtype=bool))
            log_fg_mat = jnp.where(mask, fg_mat, -jnp.inf)
            log_D = log_fg_mat + ig[:, None, :]
            max_log_D = jnp.max(log_D, axis=-1, keepdims=True)
            D_mat = jnp.exp(log_D - max_log_D)
            qk = jnp.einsum('hsd,htd->hst', qh, kh) / np.sqrt(DH)
            C = qk * D_mat
            normalizer = jnp.maximum(jnp.abs(C.sum(axis=-1, keepdims=True)), jnp.exp(-max_log_D))
            h = jnp.einsum('hst,htd->hsd', C / (normalizer + EPS), vh)
            h = h.transpose(1, 0, 2).reshape(Slen, D)
            mu = h.mean(axis=-1, keepdims=True)
            var = h.var(axis=-1, keepdims=True)
            return (h - mu) / jnp.sqrt(var + LN_EPS) * ln_scale
        return jax.vmap(lambda qq, kk, vv: _mlstm_cell(qq, kk, vv, igate_w, igate_b, fgate_w, fgate_b, ln_scale))(q, k, v)

    def _L0_ffn_ref(x, r1_w, r1_b, r2_w, w_up, w_down, a_up, a_down):
        import jax, jax.numpy as jnp
        import numpy as np
        E, G, TOPK = (32, 16, 2)
        HID, INTER, A_INTER = (512, 1024, 128)
        CAP_FACTOR = 1.25
        SCALE = 0.05

        def _stats(x):
            mean = x.mean(-1, keepdims=True)
            std = jnp.std(x, axis=-1, keepdims=True, ddof=1)
            mn = x.min(-1, keepdims=True)
            mx = x.max(-1, keepdims=True)
            l2 = jnp.linalg.norm(x, axis=-1, keepdims=True)
            sp = (jnp.abs(x) < 1e-06).astype(x.dtype).mean(-1, keepdims=True)
            return jnp.concatenate([mean, std, mn, mx, l2, sp], -1)
        B, N, C = x.shape
        xf = x.reshape(-1, C)
        T = xf.shape[0]
        cap = int(CAP_FACTOR * T / E)
        ri = jnp.concatenate([xf, _stats(xf)], -1)
        h = jax.nn.gelu(ri @ r1_w.T + r1_b, approximate=False)
        probs = jax.nn.softmax(h @ r2_w.T, -1)
        topp, topi = jax.lax.top_k(probs, TOPK)
        wnorm = topp / topp.sum(-1, keepdims=True)
        eids = jnp.arange(E)
        hit = topi[..., None] == eids
        routed = hit.any(1)
        Wc = jnp.where(hit, wnorm[..., None], 0.0).sum(1)
        score = jnp.where(routed, probs, -jnp.inf)
        idx = jnp.argsort(-score, axis=0)[:cap].T
        valid = jnp.take_along_axis(routed.T, idx, 1)
        w = jnp.take_along_axis(Wc.T, idx, 1) * valid
        xe = xf[idx]
        up = jnp.einsum('eci,eji->ecj', xe, w_up)
        gate, upv = jnp.split(up, 2, axis=-1)
        hact = jax.nn.silu(gate) * upv
        ye = jnp.einsum('ecj,eoj->eco', hact, w_down)
        out = jnp.zeros((T, C), xf.dtype).at[idx.reshape(-1)].add((w[..., None] * ye).reshape(-1, C))
        Wmask = jnp.zeros((T, E), xf.dtype).at[idx, eids[:, None]].add(w)
        gw = SCALE * Wmask.reshape(T, G, E // G).sum(-1)
        aup = jnp.einsum('tc,gjc->tgj', xf, a_up)
        ag, av = jnp.split(aup, 2, axis=-1)
        ah = jax.nn.silu(ag) * av
        ay = jnp.einsum('tgj,goj->tgo', ah, a_down)
        out = out + jnp.einsum('tg,tgo->to', gw, ay)
        return out.reshape(B, N, C)
    x = _layernorm(x + _L0_attn_ref(x, L0_attn_decay_logit, L0_attn_W, L0_attn_b, L0_attn_conv_w, L0_attn_conv_b), axis=-1)
    x = _layernorm(x + _L0_xattn_ref(x, ctx_1024, ctx_1024, L0_xattn_igate_w, L0_xattn_igate_b, L0_xattn_fgate_w, L0_xattn_fgate_b, L0_xattn_ln_scale), axis=-1)
    x = _layernorm(x + _L0_ffn_ref(x, L0_ffn_r1_w, L0_ffn_r1_b, L0_ffn_r2_w, L0_ffn_w_up, L0_ffn_w_down, L0_ffn_a_up, L0_ffn_a_down), axis=-1)
    return x

_drawn_inputs = setup_inputs


def setup_inputs(seed=0):
    import zlib

    import numpy as np

    out = dict(_drawn_inputs(seed))
    spreads = {'L0_attn_decay_logit': (0.0, 0.1),
     'L0_xattn_ln_scale': (1.0, 0.2),
     'L0_ffn_r1_b': (0.0, 0.486)}
    factors = {'L0_ffn_a_up': 8.0, 'L0_ffn_a_down': 8.0}
    for name, (base, spread) in spreads.items():
        noise = np.random.default_rng([zlib.crc32(name.encode()), seed]).standard_normal(out[name].shape)
        drawn = base * np.exp(spread * noise) if base else spread * noise
        out[name] = jnp.asarray(drawn.astype(out[name].dtype))
    for name, factor in factors.items():
        out[name] = (out[name] * factor).astype(out[name].dtype)
    return out
```

```python
from contextlib import ExitStack

import concourse.bass as bass
from concourse import mybir

F32 = mybir.dt.float32
BF16 = mybir.dt.bfloat16
I32 = mybir.dt.int32
U32 = mybir.dt.uint32
ALU = mybir.AluOpType
ACT = mybir.ActivationFunctionType
AX = mybir.AxisListType

P = 128
NB, T, D = 8, 512, 512
C = D // P
TB = T // P
NT = NB * TB
TAPS, PAD = 5, 2
NH, DH = 8, 64
NE, NG = 32, 16
RH = D // 2
RM = RH // P
INTER, AINT = 1024, 128
J = INTER // P
CAP = int(1.25 * NB * T / NE)
CAP2 = CAP - P
NTOK = NB * T
NSTAT = 6
GATE = 40
VW = DH + 1
PVN = 96
LN_EPS, CELL_EPS, SPARSE, A_SCALE = 1e-5, 1e-6, 1e-6, 0.05
AFTER = [512, 896, 1152]
AFTERW = [384, 256, 128]
SCW = 1280
MAXBIT = 29


class Batch:

    def __init__(self, t, off):
        self.t, self.off, self.slot = t, off, off % 2

    def __add__(self, k):
        return Batch(self.t, self.off + k)

    def __sub__(self, k):
        return Batch(self.t, self.off - k)

    def line(self, per, k=0):
        fixed = self.off * per + k
        return fixed if isinstance(self.t, int) else self.t * per + fixed

    def landed(self, dmas=1):
        fixed = 16 * dmas * (self.off // 2 + 1)
        return fixed if isinstance(self.t, int) else self.t * (8 * dmas) + fixed


class Steps:

    def __init__(self, sem, names, lead=0):
        self.sem, self.names, self.lead, self.next = sem, names, lead, 0
        self.index = {n: i for i, n in enumerate(names)}

    def __call__(self, name):
        assert self.names[self.next] == name, (name, self.names[self.next])
        self.next = (self.next + 1) % len(self.names)
        return self.sem

    def at(self, name, b):
        per = len(self.names)
        return self.sem, b.line(per, self.lead * per + self.index[name] + 1)

    def start(self, eng):
        if self.lead:
            eng.sem_inc(self.sem, self.lead * len(self.names))


class Room:

    def __init__(self, arena, size, used=0):
        self.arena, self.size, self.used = arena, size, used

    def take(self, *shape, dt=F32):
        n = 1
        for s in shape:
            n *= s
        words = n if dt != BF16 else (n + 1) // 2
        at, self.used = self.used, self.used + words + words % 2
        assert self.used <= self.size, (self.used, self.size)
        v = self.arena[:, at:at + words]
        if dt != F32:
            v = v.bitcast(dt)
        if len(shape) == 2:
            v = v.rearrange("p (a b) -> p a b", a=shape[0])
        if len(shape) == 3:
            v = v.rearrange("p (a b c) -> p a b c", a=shape[0], b=shape[1])
        return v


def run_pipeline(eng, step):
    full = dict(a=True, s=True, r=True, x1=True, x2=True)
    step(Batch(0, 0), **full | dict(s=False, r=False))
    step(Batch(0, 1), **full | dict(r=False))
    with eng.Fori(0, (NB - 4) // 2) as i:
        t = i * 2
        for p in range(2):
            step(Batch(t, 2 + p), **full)
    step(Batch(0, NB - 2), **full | dict(x2=False))
    step(Batch(0, NB - 1), **full | dict(x1=False, x2=False))
    step(Batch(0, NB), **full | dict(a=False, x1=False, x2=False))
    step(Batch(0, NB + 1), **full | dict(a=False, s=False, x1=False, x2=False))


def run_experts(eng, expert):
    expert(Batch(0, 0), True, False)
    expert(Batch(0, 1), False, False)
    with eng.Fori(0, (NE - 4) // 2) as i:
        t = i * 2
        for p in range(2):
            expert(Batch(t, 2 + p), False, False)
    expert(Batch(0, NE - 2), False, False)
    expert(Batch(0, NE - 1), False, True)


def decoder_kernel(nc, xT_d, kT_d, v_d, decay_d, WT_d, b_d, cw_d, cb_d, wi_d, wf_d, ib_d, fb_d, ln_d,
                   r1x_d, r1s_d, r1b_d, r2_d, wup_d, wdn_d, aup_d, adn_d, out_d):
    x2_d = nc.dram_tensor("x2_rows", (NTOK + CAP, D), F32, kind="Internal").ap()
    acc_d = nc.dram_tensor("acc_rows", (NTOK + CAP, D), F32, kind="Internal").ap()
    ctx = ExitStack()
    with ctx:
        def sem(name):
            return ctx.enter_context(nc.semaphore(name))

        every = {e: [] for e in ("tensor", "vector", "scalar", "pool")}

        def steps(name, names, lead=3):
            p = Steps(sem(name), names, lead)
            every[name.split("_")[-1]].append(p)
            return p

        held = sem("held")

        def hold(eng):
            eng.sem_inc(held, 1)

        def start(eng, name):
            for p in every[name]:
                p.start(eng)

        ROOM = 51520
        arena = ctx.enter_context(nc.sbuf_tensor("arena", [P, ROOM], F32))
        keep_t = ctx.enter_context(nc.sbuf_tensor("keep", [P, 1684], F32))
        bank = [ctx.enter_context(nc.psum_tensor(f"bank{i}", [P, 512], F32)) for i in range(8)]

        keep = Room(keep_t, 1684)
        ident = keep.take(P)
        ones = keep.take(1)
        negh = keep.take(TB)
        posh = keep.take(TB)
        sc_all = keep.take(NT // 4, 4 * NE)
        w_all = keep.take(NT, 2)
        e_all = keep.take(NT, 2)
        tid_l = keep.take(2 * NE)
        w_l = keep.take(2 * NE)
        idx_l = keep.take(2 * NE, dt=I32)
        iota_e = keep.take(NE)
        idx_g = [keep.take(2, dt=I32) for _ in range(2)]
        idx_s = [keep.take(2, dt=I32) for _ in range(2)]
        ln_st = keep.take(TB, 6)
        ln_mv = keep.take(TB, 2)
        ln_rs = keep.take(TB)

        room = Room(arena, ROOM)
        WT = room.take(C, D)
        wgq = room.take(C, GATE)
        wgk = room.take(C, GATE)
        gbias = room.take(1)
        a_dec = room.take(C)
        a_one = room.take(C)
        cw = room.take(C, TAPS)
        cb = room.take(C)
        rb = room.take(C)
        lns = room.take(D)
        r1x = room.take(C, RH)
        r1s = room.take(RH)
        r1b = room.take(RM)
        r2 = room.take(RM, NE)
        sel = room.take(NH, P, dt=BF16)
        xT = [room.take(C, T + 2 * PAD) for _ in range(2)]
        ST = room.take(C, T)
        cv = room.take(C, T)
        x1 = [room.take(TB, D) for _ in range(2)]
        qT = [room.take(C, T) for _ in range(2)]
        kT = room.take(C, T)
        kz = [room.take(2, C, T) for _ in range(2)]
        va = [room.take(TB, NH * VW + PVN - VW) for _ in range(2)]
        ND = 3
        Dm = [room.take(SCW) for _ in range(ND)]
        x2 = room.take(TB, D)
        x2T = room.take(C, T)
        hg = room.take(RM, T)
        wgv = hg[:, 0, 0:C * GATE].rearrange("p (c g) -> p c g", c=C)
        stT = room.take(T)
        zeros = room.take(2 * D)
        g_fx, g_ab, g_mn, g_ig = (room.take(T) for _ in range(4))
        g_l = g_ab
        g_lf = g_mn
        g_cs = g_fx
        g_m = room.take(T)
        g_r = g_mn
        g_m0 = room.take(T, dt=BF16)
        gm = room.take(T)
        bfs = [room.take(T, dt=BF16) for _ in range(2)]
        gcol = [room.take(TB, GATE) for _ in range(2)]
        ng = [room.take(TB, NH) for _ in range(2)]
        en = [room.take(TB, NH) for _ in range(2)]
        bn1 = room.take(TB, 6)
        mv1 = room.take(TB, 2)
        rs1 = room.take(TB)
        den = room.take(TB)
        nz = room.take(TB)
        bn2 = room.take(TB, 6)
        mv2 = room.take(TB, 2)
        rs2 = room.take(TB)
        bn3 = room.take(TB, 6)
        mv3 = room.take(TB, 2)
        rs3 = room.take(TB)
        bnr = room.take(TB, 6)
        mvr = room.take(TB, 2)
        vr = room.take(2, TB)
        st6 = room.take(TB, NSTAT)
        junk = zeros.bitcast(BF16).rearrange("p (a d) -> p a d", a=TB)
        zeros = zeros[:, 0:D]
        lg = room.take(TB, NE)
        nmx = room.take(TB)
        pr = room.take(TB, NE)
        top8 = room.take(TB, 8)
        at8 = room.take(TB, 8, dt=U32)
        ex2 = room.take(TB, 2)
        oh0 = room.take(TB, NE)
        oh1 = room.take(TB, NE)
        wsum = room.take(TB)

        Wb = bank[0:2]
        Tb = bank[2]
        Sb = bank[3:5]
        Bb = bank[5]
        Pb = bank[6:8]

        ld_c = sem("ld_consts")
        ld_x = [sem(f"ld_x{i}") for i in range(2)]
        ld_k = sem("ld_k")
        ld_z = [sem(f"ld_kz{i}") for i in range(2)]
        ld_v = [sem(f"ld_v{i}") for i in range(2)]
        st_x2 = sem("st_x2")
        st_acc = sem("st_acc")
        st_dum = sem("st_dummy_rows")

        cs_v = steps("const_vector", ["zero", "misc", "dec1", "dec2", "gkv", "tap"], 0)
        cs_a = steps("const_scalar", ["dec"], 0)
        cs_p = steps("const_pool", ["ident0", "ident"] + [f"sel{q}" for q in range(4)] + ["iota"], 0)
        re_a = steps("ret_scalar", [x for c in range(C) for x in (f"u{c}", f"cv{c}")])
        re_v = steps("ret_vector", [x for c in range(C) for x in
                                    [f"scan{c}"] + [f"tap{k}_{c}" for k in range(TAPS - 1)]])
        re_t = steps("ret_tensor", [f"w{tb}" for tb in range(TB)])
        n1_a = steps("ln1_scalar", [f"raw{tb}" for tb in range(TB)])
        n1_v = steps("ln1_vector", [f"bn{tb}" for tb in range(TB)] + ["aggr"] + [f"out{tb}" for tb in range(TB)])
        n1_p = steps("ln1_pool", ["eps", "rstd"])
        qt_t = steps("qT_tensor", [f"t{tb}" for tb in range(TB)])
        qt_a = steps("qT_scalar", [f"q{tb}" for tb in range(TB)])
        ga_t = steps("gate_tensor", ["gates", "cols"])
        ga_a = steps("gate_scalar", ["ig", "fx", "exp", "log", "hi", "m0", "mid", "gcol", "ng", "en"])
        ga_v = steps("gate_vector", ["abs", "min", "logf", "cum", "g", "max", "neg", "r1", "lo"])
        at_t = steps("att_tensor", [x for h in range(NH) for x in
                                    (f"bc{h}", f"s{h}_0", f"s{h}_1", f"s{h}_2")] )
        pv_t = steps("pv_tensor", [f"pv{h}" for h in range(NH)])
        at_a = steps("att_scalar", [x for h in range(NH) for x in (f"relu{h}", f"exp{h}")])
        at_p = steps("att_pool", [f"mask{h}" for h in range(NH)])
        at_v = steps("att_vector", [f"mul{h}_{i}" for h in range(NH) for i in range(3)])
        ev_v = steps("ev_vector", [x for h in range(NH) for x in (f"neg{h}", f"den{h}", f"eps{h}", f"rec{h}", f"out{h}")])
        l2_v = steps("ln2_vector", ["bn2", "aggr2", "scaled", "sum", "bn3", "aggr3"] +
                     [f"out{tb}" for tb in range(TB)])
        l2_p = steps("ln2_pool", ["eps2", "rstd2", "eps3", "rstd3"])
        ro_t = steps("router_tensor", [f"x{tb}" for tb in range(TB)] + ["st", "h0", "h1", "lg"])
        ro_a = steps("router_scalar", [f"x{tb}" for tb in range(TB)] + ["st", "h0", "h1", "lg", "exp"])
        ro_v = steps("router_vector", ["bn", "aggr", "sq", "sum", "vars", "above", "cnt", "stats",
                                       "lmax", "lsub", "lsum", "lrec", "prob", "top", "at",
                                       "sum2", "rec2", "oh", "ohs", "save"])
        ro_p = steps("router_pool", ["std", "l2"])
        b0 = Batch(0, 0)
        bl = Batch(0, NB - 1)

        xc = [t[:, :, PAD:PAD + T] for t in xT]

        room2 = Room(arena, ROOM)
        wu = [room2.take(C, 2 * INTER) for _ in range(2)]
        wd = [room2.take(J, D) for _ in range(2)]
        au = [room2.take(C, 2 * AINT) for _ in range(2)]
        ad = [room2.take(D) for _ in range(2)]
        late = room2.used
        scT = room2.take(NT // 4, P)
        cmpb = room2.take(NT // 4, P)
        thr = room2.take(1, dt=I32)
        lo = room2.take(1, dt=I32)
        bit = room2.take(1, dt=I32)
        cnt = room2.take(1)
        need = room2.take(1)
        gt = room2.take(NT // 4, P)
        eq = room2.take(NT // 4, P)
        pos = room2.take(NT // 4, P)
        base = room2.take(1)
        blk = room2.take(P)
        low = room2.take(P)
        posT = room2.take(NT, NE)
        ohk = room2.take(NT, NE)
        emp = room2.take(2 * NE)
        off = room2.take(1)
        slot = room2.take(2, NT)
        shi = room2.take(2, NT)
        slo = room2.take(2, NT)
        tid = room2.take(NT)
        iota_h = room2.take(2 * NE)
        iota_l = room2.take(P)
        iota_s = room2.take(2 * NE)
        Lh = [room2.take(P) for _ in range(2)]
        Hh = [room2.take(2, 2 * NE) for _ in range(2)]
        room3 = Room(arena, ROOM, late)
        xg = [room3.take(2, D) for _ in range(2)]
        xeT = room3.take(C, CAP)
        sg = [room3.take(CAP) for _ in range(2)]
        hact = room3.take(J + 1, CAP)
        yT = room3.take(C, CAP)
        yy = [room3.take(2, D) for _ in range(2)]
        room4 = Room(arena, ROOM)
        fin = [room4.take(TB, D) for _ in range(2)]

        Ub = bank[0:2]
        Db = bank[2:4]
        Xb = bank[4:6]
        Yb = bank[6:8]

        ld_wu = [sem(f"ld_wup{i}") for i in range(2)]
        ld_wd = [sem(f"ld_wdown{i}") for i in range(2)]
        ld_au = [sem(f"ld_aup{i}") for i in range(2)]
        ld_ad = [sem(f"ld_adown{i}") for i in range(2)]
        ld_g = [sem(f"gathered{i}") for i in range(2)]
        st_y = sem("scattered")
        NSEL = MAXBIT + 1
        se_v = steps("sel_vector", ["scT0", "scT1", "lo", "thr"] +
                     [x for i in range(NSEL) for x in (f"cmp{i}", f"bit{i}", f"lo{i}", f"thr{i}")] +
                     ["gt", "need", "off", "eqthr", "eq", "eqscan", "eqoff", "eqok", "eqsel", "sel", "scan",
                      "selbase", "masked", "posT0", "posT1", "oh0", "pr0", "s0", "oh1", "pr1", "s1",
                      "hi", "lo_", "hi2"], 0)
        se_p = steps("sel_pool", ["blk0", "blk1", "low1", "blk2", "blk3", "low2", "blk4", "blk5", "low3", "blk6",
                                  "blk7", "iotas"], 0)
        se_t = steps("sel_tensor", ["scT0", "scT1"] + [f"cnt{i}" for i in range(NSEL)] +
                     ["gtc", "eqo", "selo", "posT0", "posT1"], 0)
        li_v = steps("list_vector", [f"w{i}" for i in range(2 * NT)], 0)
        li_t = steps("list_tensor", [f"m{i}" for i in range(2 * NT)], 0)
        lf_v = steps("listfin_vector", ["tid", "w", "empty", "fill", "idx"], 0)
        up_t = steps("up_tensor", [f"up{j}" for j in range(J + 1)], 2)
        up_a = steps("up_scalar", [f"silu{j}" for j in range(J + 1)], 2)
        up_v = steps("up_vector", [f"mul{j}" for j in range(J + 1)], 2)
        xr_t = steps("rowsin_tensor", ["x0", "x1"], 2)
        xr_a = steps("rowsin_scalar", ["x0", "x1"], 2)
        dn_t = steps("down_tensor", ["d0", "d1"], 2)
        dn_a = steps("down_scalar", ["d0", "d1"], 2)
        yr_t = steps("rowsout_tensor", ["y0", "y1"], 2)
        yr_v = steps("rowsout_vector", ["y0", "y1"], 2)
        ig_p = steps("gatherindex_pool", ["copy"])
        is_p = steps("scatterindex_pool", ["copy"])
        ld_f = [sem(f"ld_fin{i}") for i in range(2)]
        st_f = [sem(f"st_fin{i}") for i in range(2)]
        fi_v = steps("fin_vector", ["bn", "aggr", "out"], 2)
        fi_p = steps("fin_pool", ["eps", "rstd"], 2)

        NCONST = 18
        block = ctx.enter_context(nc.Block())

        @block.sync
        def _(sp):
            sp.wait_ge(*cs_v.at("misc", b0))
            for dst, src in ((WT, WT_d), (wgq[:, :, 0:NH], wi_d[:, 0:C]), (wgk[:, :, 0:NH], wi_d[:, C:2 * C]),
                             (wgv[:, :, 0:NH], wi_d[:, 2 * C:]), (wgq[:, :, 32:GATE], wf_d[:, 0:C]),
                             (wgk[:, :, 32:GATE], wf_d[:, C:2 * C]), (wgv[:, :, 32:GATE], wf_d[:, 2 * C:]),
                             (gbias[0:NH], ib_d), (gbias[32:GATE], fb_d), (a_dec, decay_d), (cw, cw_d),
                             (cb, cb_d), (rb, b_d), (lns, ln_d.to_broadcast([P, D])), (r1x, r1x_d),
                             (r1s[0:NSTAT], r1s_d), (r1b, r1b_d), (r2, r2_d)):
                sp.dma_start(dst, src).then_inc(ld_c, 16)

            def load_x(b):
                sp.wait_ge(*re_v.at(f"tap{TAPS - 2}_{C - 1}", b - 2))
                sp.dma_start(xc[b.slot], xT_d[b.line(1)]).then_inc(ld_x[b.slot], 16)

            def load_context(b):
                sp.wait_ge(*ga_t.at("gates", b - 1))
                sp.dma_start(kT, kT_d[b.line(1)]).then_inc(ld_k, 16)
                sp.wait_ge(*pv_t.at(f"pv{NH - 1}", b - 2))
                for r in range(2):
                    half = slice(r * DH, (r + 1) * DH)
                    sp.dma_start(kz[b.slot][half, r], kT_d[b.line(1), half]).then_inc(ld_z[b.slot], 16)
                for tb in range(TB):
                    dst = va[b.slot][:, tb, 0:NH * VW].rearrange("p (h w) -> p h w", h=NH)[:, :, 0:DH]
                    sp.dma_start(dst, v_d[b.line(1), :, tb]).then_inc(ld_v[b.slot], 16)

            def store_x2(b):
                sp.wait_ge(*l2_v.at(f"out{TB - 1}", b))
                for rows, done in ((x2_d, st_x2), (acc_d, st_acc)):
                    dst = rows[0:NTOK].rearrange("(n a p) d -> n p a d", a=TB, p=P)[b.line(1)]
                    sp.dma_start(dst, x2).then_inc(done, 16)

            def step(n, a, s, r, x1, x2):
                if r:
                    store_x2(n - 2)
                if a:
                    load_context(n)
                if x2:
                    load_x(n + 2)

            load_x(b0)
            load_x(b0 + 1)
            for rows in (x2_d, acc_d):
                sp.dma_start(rows[NTOK:NTOK + P], zeros).then_inc(st_dum, 16)
                sp.dma_start(rows[NTOK + P:], zeros[0:CAP2]).then_inc(st_dum, 16)
            run_pipeline(sp, step)

            sp.wait_ge(*ro_v.at("save", bl))
            sp.wait_ge(*ro_t.at("lg", bl))
            sp.wait_ge(st_x2, 16 * NB)
            sp.wait_ge(st_acc, 16 * NB)

            def load_expert(e, pair):
                s = e.slot
                sp.wait_ge(*up_t.at(f"up{J - 1}", e - 2))
                sp.dma_start(wu[s], wup_d[e.line(1)]).then_inc(ld_wu[s], 16)
                sp.wait_ge(*up_t.at(f"up{J}", e - 2))
                sp.dma_start(au[s], aup_d[pair]).then_inc(ld_au[s], 16)
                sp.wait_ge(*dn_t.at("d1", e - 2))
                sp.dma_start(wd[s], wdn_d[e.line(1)]).then_inc(ld_wd[s], 16)
                sp.dma_start(ad[s], adn_d[pair]).then_inc(ld_ad[s], 16)

            for p in range(2):
                load_expert(Batch(0, p), 0)
            with sp.Fori(0, NE // 2 - 1) as i:
                t, pair = i * 2, i + 1
                for p in range(2):
                    load_expert(Batch(t, 2 + p), pair)

            def load_fin(b):
                src = acc_d[0:NTOK].rearrange("(n a p) d -> n p a d", a=TB, p=P)[b.line(1)]
                sp.dma_start(fin[b.slot], src).then_inc(ld_f[b.slot], 16)

            def store_fin(b):
                sp.wait_ge(*fi_v.at("out", b))
                dst = out_d[b.line(1)].rearrange("(a p) d -> p a d", p=P)
                sp.dma_start(dst, fin[b.slot]).then_inc(st_f[b.slot], 16)

            sp.wait_ge(st_y, 32 * NE)
            load_fin(Batch(0, 0))
            load_fin(Batch(0, 1))
            with sp.Fori(0, (NB - 2) // 2) as i:
                t = i * 2
                for p in range(2):
                    b = Batch(t, p)
                    store_fin(b)
                    sp.wait_ge(st_f[p], b.landed())
                    load_fin(b + 2)
            for p in range(2):
                store_fin(Batch(0, NB - 2 + p))
            for p in range(2):
                sp.wait_ge(st_f[p], Batch(0, NB - 2 + p).landed())

        @block.tensor
        def _(pe):
            start(pe, "tensor")
            pe.wait_ge(ld_c, 16 * NCONST)
            pe.wait_ge(*cs_p.at("iota", b0))
            pe.wait_ge(*cs_v.at("gkv", b0))

            def broadcast_max(b, h):
                if h == 0:
                    pe.wait_ge(*ga_v.at("lo", b))
                    pe.wait_ge(*ga_a.at("mid", b))
                    pe.wait_ge(*at_a.at(f"exp{NH - 1}", b - 1))
                else:
                    pe.wait_ge(*at_a.at(f"exp{h - 1}", b))
                pe.matmul(Bb[:, :], sel[:, h, :], bfs[b.slot], start=True, stop=True).then_inc(at_t(f"bc{h}"), 1)

            def retention(b):
                pe.wait_ge(*re_v.at(f"tap{TAPS - 2}_{C - 1}", b))
                for tb in range(TB):
                    w = Wb[tb % 2]
                    if tb < 2:
                        pe.wait_ge(*qt_a.at(f"q{tb + 2}", b - 1))
                        pe.wait_ge(*ro_a.at(f"h{tb}", b - 3))
                    else:
                        pe.wait_ge(*n1_a.at(f"raw{tb - 2}", b))
                    rows = slice(tb * P, (tb + 1) * P)
                    for c in range(C):
                        pe.matmul(w[:, :], ST[:, c, rows], WT[:, c, :], start=(c == 0), stop=False)
                    for c in range(C):
                        m = pe.matmul(w[:, c * P:(c + 1) * P], cv[:, c, rows], ident, start=False, stop=(c == C - 1))
                    m.then_inc(re_t(f"w{tb}"), 1)

            def queries(b):
                for tb in range(TB):
                    w = Wb[tb % 2]
                    pe.wait_ge(*n1_v.at(f"out{tb}", b))
                    if tb >= 2:
                        pe.wait_ge(*qt_a.at(f"q{tb - 2}", b))
                    else:
                        pe.wait_ge(*ro_a.at(f"h{tb}", b - 2))
                    for c in range(C):
                        m = pe.transpose(w[:, c * P:(c + 1) * P], x1[b.slot][:, tb, c * P:(c + 1) * P], ident)
                    m.then_inc(qt_t(f"t{tb}"), 1)

            def gates(b):
                pe.wait_ge(*qt_a.at(f"q{TB - 1}", b))
                pe.wait_ge(ld_k, b.line(16, 16))
                pe.wait_ge(*ro_a.at("lg", b - 2))
                pe.wait_ge(*ga_a.at("gcol", b - 1))
                for c in range(C):
                    pe.matmul(Tb[0:GATE, :], wgq[:, c, :], qT[b.slot][:, c, :], start=(c == 0), stop=False)
                for c in range(C):
                    m = pe.matmul(Tb[0:GATE, :], wgk[:, c, :], kT[:, c, :], start=False, stop=(c == C - 1))
                m.then_inc(ga_t("gates"), 1)

            def gate_columns(b):
                pe.wait_ge(*ga_v.at("neg", b))
                hold(pe)
                for tb in range(TB):
                    m = pe.transpose(Tb[:, tb * GATE:(tb + 1) * GATE], gm[0:GATE, tb * P:(tb + 1) * P],
                                     ident[0:GATE, 0:GATE])
                m.then_inc(ga_t("cols"), 1)

            def scores(b, h):
                if h == 0:
                    pe.wait_ge(ld_z[b.slot], b.landed(2))
                own = [(tb * P, P, tb, tb) for tb in range(TB)]
                rest = [(AFTER[tb] - AFTER[min(tb, 1)], AFTERW[tb], tb, tb + 1) for tb in range(TB - 1)]
                for i, parts in enumerate((own, rest[:1], rest[1:])):
                    k = 3 * h + i
                    if k >= 2:
                        pe.wait_ge(*at_v.at(f"mul{(k - 2) // 3}_{(k - 2) % 3}", b))
                    else:
                        pe.wait_ge(*at_v.at(f"mul{NH - 1}_{1 + k}", b - 1))
                    for at, n, tb, q in parts:
                        m = pe.matmul(Sb[k % 2][:, at:at + n], kz[b.slot][:, h % 2, h // 2, tb * P:(tb + 1) * P],
                                      qT[b.slot][:, h // 2, q * P:q * P + n], start=True, stop=True)
                    m.then_inc(at_t(f"s{h}_{i}"), 1)

            def values(b, h):
                if h == 0:
                    pe.wait_ge(ld_v[b.slot], b.landed(TB))
                pe.wait_ge(*at_v.at(f"mul{h}_2", b))
                if h >= 2:
                    pe.wait_ge(*ev_v.at(f"out{h - 2}", b))
                else:
                    pe.wait_ge(*ev_v.at(f"out{NH - 2 + h}", b - 1))
                for sb in range(TB):
                    for tb in range(sb + 1):
                        at = tb * P if sb == tb else AFTER[tb] + (sb - tb - 1) * P
                        m = pe.matmul(Pb[h % 2][:, sb * PVN:(sb + 1) * PVN], Dm[h % ND][:, at:at + P],
                                      va[b.slot][:, tb, h * VW:h * VW + PVN], start=(tb == 0), stop=(tb == sb))
                m.then_inc(pv_t(f"pv{h}"), 1)

            def router_in(b, before):
                for tb in range(TB):
                    w = Wb[tb % 2]
                    pe.wait_ge(*l2_v.at(f"out{tb}", b))
                    if tb >= 2:
                        pe.wait_ge(*ro_a.at(f"x{tb - 2}", b))
                    elif before:
                        pe.wait_ge(*n1_a.at(f"raw{tb + 2}", b + 2))
                    else:
                        pe.wait_ge(*ro_a.at(f"h{tb}", b - 1))
                        pe.wait_ge(*qt_a.at(f"q{tb + 2}", bl))
                    for c in range(C):
                        m = pe.transpose(w[:, c * P:(c + 1) * P], x2[:, tb, c * P:(c + 1) * P], ident)
                    m.then_inc(ro_t(f"x{tb}"), 1)
                pe.wait_ge(*ro_v.at("stats", b))
                if before:
                    pe.wait_ge(*ga_a.at("gcol", b + 1))
                else:
                    pe.wait_ge(*ga_a.at("gcol", bl))
                    pe.wait_ge(*ro_a.at("lg", b - 1))
                for tb in range(TB):
                    m = pe.transpose(Tb[0:NSTAT, tb * P:(tb + 1) * P], st6[:, tb, :], ident)
                m.then_inc(ro_t("st"), 1)

            def router_out(b):
                for k in range(RM):
                    pe.wait_ge(*ro_a.at(f"x{TB - 1}", b))
                    for c in range(C):
                        pe.matmul(Wb[k][:, :], r1x[:, c, k * P:(k + 1) * P], x2T[:, c, :], start=(c == 0), stop=False)
                    pe.wait_ge(*ro_a.at("st", b))
                    pe.matmul(Wb[k][:, :], r1s[:, k * P:(k + 1) * P], stT, start=False, stop=True)\
                        .then_inc(ro_t(f"h{k}"), 1)
                pe.wait_ge(*ro_a.at("h1", b))
                for tb in range(TB):
                    for k in range(RM):
                        m = pe.matmul(Tb[:, tb * NE:(tb + 1) * NE], hg[:, k, tb * P:(tb + 1) * P], r2[:, k, :],
                                      start=(k == 0), stop=(k == RM - 1))
                m.then_inc(ro_t("lg"), 1)

            def step(n, a, s, r, x1, x2):
                if s:
                    broadcast_max(n - 1, 0)
                if a:
                    retention(n)
                if r:
                    router_in(n - 2, a)
                if s:
                    scores(n - 1, 0)
                if r:
                    router_out(n - 2)
                for h in range(NH):
                    if s:
                        if h + 1 < NH:
                            broadcast_max(n - 1, h + 1)
                            scores(n - 1, h + 1)
                        values(n - 1, h)
                    if h == 2 and a:
                        queries(n)
                    if h == 3 and a:
                        gates(n)
                if a:
                    gate_columns(n)

            run_pipeline(pe, step)

            pe.wait_ge(*ro_v.at("save", bl))
            for half in range(2):
                for k in range(4):
                    m = pe.transpose(Wb[half][:, k * P:(k + 1) * P], sc_all[:, half * 4 + k, :], ident)
                m.then_inc(se_t(f"scT{half}"), 1)
            pe.wait_ge(*se_p.at("iotas", b0))
            for i in range(NSEL):
                pe.wait_ge(*se_v.at(f"cmp{i}", b0))
                pe.matmul(Tb[:, 0:1], blk, cnt, start=True, stop=True).then_inc(se_t(f"cnt{i}"), 1)
            last = slice(P - 1, P)
            for name, w, after, col in (("gtc", blk, "gt", cnt), ("eqo", low, "eqscan", cmpb[:, NT // 4 - 1, last]),
                                        ("selo", low, "scan", pos[:, NT // 4 - 1, last])):
                pe.wait_ge(*se_v.at(after, b0))
                pe.matmul(Tb[:, 0:1], w, col, start=True, stop=True).then_inc(se_t(name), 1)
            pe.wait_ge(*se_v.at("masked", b0))
            for half in range(2):
                for k in range(4):
                    m = pe.transpose(Wb[half][:, k * P:(k + 1) * P], pos[:, half * 4 + k, :], ident)
                m.then_inc(se_t(f"posT{half}"), 1)
            for i in range(2 * NT):
                pe.wait_ge(*li_v.at(f"w{i}", b0))
                pe.matmul(Tb[:, 0:4 * NE], Lh[i % 2], Hh[i % 2].rearrange("p a b -> p (a b)"),
                          start=(i == 0), stop=(i == 2 * NT - 1)).then_inc(li_t(f"m{i}"), 1)

            def rows_in(e):
                pe.wait_ge(ld_g[e.slot], e.landed(2))
                for k in range(2):
                    pe.wait_ge(*xr_a.at(f"x{k}", e - 1))
                    for c in range(2):
                        ch = slice((2 * k + c) * P, (2 * k + c + 1) * P)
                        pe.transpose(Xb[k][:, c * CAP:c * CAP + P], xg[e.slot][:, 0, ch], ident)
                        m = pe.transpose(Xb[k][:, c * CAP + P:(c + 1) * CAP], xg[e.slot][0:CAP2, 1, ch],
                                         ident[0:CAP2, 0:CAP2])
                    m.then_inc(xr_t(f"x{k}"), 1)

            def up(e, j):
                if j == 0:
                    pe.wait_ge(ld_wu[e.slot], e.landed())
                    pe.wait_ge(*xr_a.at("x1", e))
                if j == J:
                    pe.wait_ge(ld_au[e.slot], e.landed())
                if j < 2:
                    pe.wait_ge(*up_v.at(f"mul{J - 1 + j}", e - 1))
                else:
                    pe.wait_ge(*up_v.at(f"mul{j - 2}", e))
                u = Ub[(e.slot * (J + 1) + j) % 2]
                for g in range(2):
                    for c in range(C):
                        w = wu[e.slot][:, c, g * INTER + j * P:g * INTER + (j + 1) * P] if j < J else \
                            au[e.slot][:, c, g * AINT:(g + 1) * AINT]
                        m = pe.matmul(u[:, g * CAP:(g + 1) * CAP], w, xeT[:, c, :], start=(c == 0), stop=(c == C - 1))
                m.then_inc(up_t(f"up{j}"), 1)

            def down(e):
                pe.wait_ge(ld_wd[e.slot], e.landed())
                pe.wait_ge(ld_ad[e.slot], e.landed())
                pe.wait_ge(*up_v.at(f"mul{J}", e))
                for k in range(2):
                    pe.wait_ge(*dn_a.at(f"d{k}", e - 1))
                    for c in range(2):
                        ch = slice((2 * k + c) * P, (2 * k + c + 1) * P)
                        for j in range(J + 1):
                            w = wd[e.slot][:, j, ch] if j < J else ad[e.slot][:, ch]
                            m = pe.matmul(Db[k][:, c * CAP:(c + 1) * CAP], w, hact[:, j, :], start=(j == 0), stop=(j == J))
                    m.then_inc(dn_t(f"d{k}"), 1)

            def rows_out(e):
                pe.wait_ge(*dn_a.at("d1", e))
                for k in range(2):
                    pe.wait_ge(*yr_v.at(f"y{k}", e - 1))
                    for c in range(C):
                        if k == 0:
                            m = pe.transpose(Yb[0][:, c * P:(c + 1) * P], yT[:, c, 0:P], ident)
                        else:
                            m = pe.transpose(Yb[1][0:CAP2, c * P:(c + 1) * P], yT[:, c, P:CAP], ident)
                    m.then_inc(yr_t(f"y{k}"), 1)

            def expert(e, first, last_):
                up(e, 0)
                if not first:
                    rows_out(e - 1)
                for j in range(1, J + 1):
                    up(e, j)
                if not last_:
                    rows_in(e + 1)
                down(e)

            rows_in(b0)
            run_experts(pe, expert)
            rows_out(Batch(0, NE - 1))

        @block.scalar
        def _(act):
            start(act, "scalar")
            act.wait_ge(ld_c, 16 * NCONST)
            act.activation(a_dec, a_dec, ACT.Exp, scale=-1.0).then_inc(cs_a("dec"), 1)
            act.wait_ge(*cs_v.at("tap", b0))

            def inputs(b, c):
                if c == 0:
                    act.wait_ge(ld_x[b.slot], b.landed())
                    act.wait_ge(*re_t.at(f"w{TB - 1}", b - 1))
                act.activation(ST[:, c, :], xc[b.slot][:, c, :], ACT.Identity, scale=a_one[:, c:c + 1])\
                    .then_inc(re_a(f"u{c}"), 1)
                act.activation(cv[:, c, :], xc[b.slot][:, c, :], ACT.Identity, scale=cw[:, c, PAD:PAD + 1],
                               bias=cb[:, c:c + 1]).then_inc(re_a(f"cv{c}"), 1)

            def raw_rows(b):
                act.wait_ge(*l2_v.at("sum", b - 2))
                act.wait_ge(*qt_t.at(f"t{TB - 1}", b - 2))
                for tb in range(TB):
                    act.wait_ge(*re_t.at(f"w{tb}", b))
                    act.activation(x1[b.slot][:, tb, :], Wb[tb % 2][:, :], ACT.Copy).then_inc(n1_a(f"raw{tb}"), 1)

            def queries(b):
                act.wait_ge(*at_t.at(f"s{NH - 1}_2", b - 2))
                for tb in range(TB):
                    act.wait_ge(*qt_t.at(f"t{tb}", b))
                    act.activation(qT[b.slot][:, :, tb * P:(tb + 1) * P],
                                   Wb[tb % 2][:, :].rearrange("p (c t) -> p c t", c=C), ACT.Copy)\
                        .then_inc(qt_a(f"q{tb}"), 1)

            def gates_1(b):
                act.wait_ge(*ga_v.at("lo", b - 1))
                act.wait_ge(*ga_t.at("gates", b))
                act.activation(g_ig[0:NH], Tb[0:NH, :], ACT.Identity, bias=gbias[0:NH]).then_inc(ga_a("ig"), 1)
                act.activation(g_fx[0:NH], Tb[32:GATE, :], ACT.Identity, bias=gbias[32:GATE]).then_inc(ga_a("fx"), 1)

            def gates_2(b):
                act.wait_ge(*ga_v.at("abs", b))
                act.activation(g_ab[0:NH], g_ab[0:NH], ACT.Exp, scale=-1.0).then_inc(ga_a("exp"), 1)
                act.wait_ge(*ga_a.at("exp", b))
                act.activation(g_l[0:NH], g_ab[0:NH], ACT.Ln, bias=1.0).then_inc(ga_a("log"), 1)

            def gates_3(b):
                act.wait_ge(*ga_v.at("max", b))
                act.wait_ge(*at_t.at(f"bc{NH - 1}", b - 2))
                act.activation(bfs[b.slot][0:NH], g_m[0:NH], ACT.Copy, scale=-1.0).then_inc(ga_a("hi"), 1)
                act.wait_ge(*ga_v.at("r1", b))
                act.activation(g_m0[0:NH], g_r[0:NH], ACT.Copy).then_inc(ga_a("m0"), 1)
                act.activation(bfs[b.slot][32:GATE], g_r[0:NH], ACT.Copy).then_inc(ga_a("mid"), 1)

            def gates_4(b):
                act.wait_ge(*ga_t.at("cols", b))
                act.wait_ge(*ev_v.at(f"den{NH - 1}", b - 2))
                act.wait_ge(*at_a.at(f"exp{NH - 1}", b - 2))
                act.activation(gcol[b.slot], Tb[:, 0:TB * GATE].rearrange("p (a g) -> p a g", a=TB), ACT.Copy)\
                    .then_inc(ga_a("gcol"), 1)
                act.wait_ge(*ga_a.at("gcol", b))
                act.activation(ng[b.slot], gcol[b.slot][:, :, 0:NH], ACT.Copy, scale=-1.0).then_inc(ga_a("ng"), 1)
                act.activation(en[b.slot], gcol[b.slot][:, :, 32:GATE], ACT.Exp).then_inc(ga_a("en"), 1)

            def decays(b, h):
                act.wait_ge(*at_t.at(f"bc{h}", b))
                if h >= ND:
                    act.wait_ge(*pv_t.at(f"pv{h - ND}", b))
                else:
                    former = max(k for k in range(NH) if k % ND == h)
                    act.wait_ge(*pv_t.at(f"pv{former}", b - 1))
                if h == 0:
                    act.wait_ge(*ga_a.at("en", b))
                for tb in range(TB):
                    m = act.activation(Dm[h % ND][:, tb * P:(tb + 1) * P], Bb[:, tb * P:(tb + 1) * P], ACT.Relu,
                                       scale=-1.0, bias=ng[b.slot][:, tb, h:h + 1])
                m.then_inc(at_a(f"relu{h}"), 1)
                for tb in range(TB - 1):
                    act.activation(Dm[h % ND][:, AFTER[tb]:AFTER[tb] + AFTERW[tb]], Bb[:, (tb + 1) * P:], ACT.Exp,
                                   bias=gcol[b.slot][:, tb, h:h + 1])
                act.wait_ge(*at_a.at(f"relu{h}", b))
                act.activation(Dm[h % ND][:, 0:TB * P], Dm[h % ND][:, 0:TB * P], ACT.Exp, scale=-1.0)\
                    .then_inc(at_a(f"exp{h}"), 1)

            def router_1(b):
                act.wait_ge(*ro_t.at("h1", b - 1))
                for tb in range(TB):
                    act.wait_ge(*ro_t.at(f"x{tb}", b))
                    act.activation(x2T[:, :, tb * P:(tb + 1) * P],
                                   Wb[tb % 2][:, :].rearrange("p (c t) -> p c t", c=C), ACT.Copy)\
                        .then_inc(ro_a(f"x{tb}"), 1)
                act.wait_ge(*ro_t.at("st", b))
                act.activation(stT[0:NSTAT], Tb[0:NSTAT, :], ACT.Copy).then_inc(ro_a("st"), 1)

            def router_2(b):
                act.wait_ge(*ro_t.at("lg", b - 1))
                for k in range(RM):
                    act.wait_ge(*ro_t.at(f"h{k}", b))
                    act.activation(hg[:, k, :], Wb[k][:, :], ACT.Gelu, bias=r1b[:, k:k + 1])\
                        .then_inc(ro_a(f"h{k}"), 1)

            def router_3(b):
                act.wait_ge(*ro_t.at("lg", b))
                act.wait_ge(*ro_v.at("lsub", b - 1))
                act.activation(lg, Tb[:, 0:TB * NE].rearrange("p (a e) -> p a e", a=TB), ACT.Copy)\
                    .then_inc(ro_a("lg"), 1)

            def router_4(b):
                act.wait_ge(*ro_v.at("lsub", b))
                act.activation(pr, pr, ACT.Exp).then_inc(ro_a("exp"), 1)

            def step(n, a, s, r, x1, x2):
                if s:
                    decays(n - 1, 0)
                if a:
                    raw_rows(n)
                if r:
                    router_1(n - 2)
                    router_2(n - 2)
                    router_3(n - 2)
                for h in range(NH):
                    if s and h + 1 < NH:
                        decays(n - 1, h + 1)
                    if h < C and x1:
                        inputs(n + 1, h)
                    if h == 0 and r:
                        router_4(n - 2)
                    if a:
                        if h == 2:
                            queries(n)
                        if h == 3:
                            gates_1(n)
                        if h == 4:
                            gates_2(n)
                        if h == 6:
                            gates_3(n)
                if a:
                    gates_4(n)

            for c in range(C):
                inputs(b0, c)
            run_pipeline(act, step)

            def rows_in(e):
                act.wait_ge(*up_t.at(f"up{J}", e - 1))
                for k in range(2):
                    act.wait_ge(*xr_t.at(f"x{k}", e))
                    act.activation(xeT[:, 2 * k:2 * k + 2, :],
                                   Xb[k][:, 0:2 * CAP].rearrange("p (c t) -> p c t", c=2), ACT.Copy)\
                        .then_inc(xr_a(f"x{k}"), 1)

            def expert(e, first, last):
                for j in range(J + 1):
                    act.wait_ge(*up_t.at(f"up{j}", e))
                    if j >= 2:
                        act.wait_ge(*up_v.at(f"mul{j - 2}", e))
                    else:
                        act.wait_ge(*up_v.at(f"mul{J - 1 + j}", e - 1))
                    k = (e.slot * (J + 1) + j) % 2
                    act.activation(sg[k], Ub[k][:, 0:CAP], ACT.Silu).then_inc(up_a(f"silu{j}"), 1)
                if not last:
                    rows_in(e + 1)
                act.wait_ge(*yr_t.at("y1", e - 1))
                for k in range(2):
                    act.wait_ge(*dn_t.at(f"d{k}", e))
                    act.activation(yT[:, 2 * k:2 * k + 2, :],
                                   Db[k][:, 0:2 * CAP].rearrange("p (c t) -> p c t", c=2), ACT.Copy)\
                        .then_inc(dn_a(f"d{k}"), 1)

            rows_in(b0)
            run_experts(act, expert)

        @block.vector
        def _(dve):
            start(dve, "vector")
            for t in (xT[0], xT[1], kz[0], kz[1], wgq, wgk, wgv):
                dve.memset(t, 0.0)
            for t in va:
                dve.memset(t, 0.0)
            for t in (gm, stT, r1s, bfs[0], bfs[1], zeros):
                dve.memset(t, 0.0)
            dve.memset(negh, -0.5)
            dve.memset(posh, 0.5).then_inc(cs_v("zero"), 1)
            dve.wait_ge(*cs_v.at("zero", b0))
            for t in va:
                dve.memset(t[:, :, 0:NH * VW].rearrange("p a (h w) -> p a h w", h=NH)[:, :, :, DH:VW], 1.0)
            dve.memset(ones, 1.0).then_inc(cs_v("misc"), 1)
            dve.wait_ge(ld_c, 16 * NCONST)
            dve.wait_ge(*cs_a.at("dec", b0))
            dve.tensor_scalar(a_dec, a_dec, 1.0, None, ALU.add).then_inc(cs_v("dec1"), 1)
            dve.wait_ge(*cs_v.at("dec1", b0))
            dve.reciprocal(a_dec, a_dec).then_inc(cs_v("dec2"), 1)
            dve.wait_ge(*cs_v.at("dec2", b0))
            dve.tensor_scalar(a_one, a_dec, -1.0, 1.0, ALU.mult, ALU.add)
            dve.tensor_tensor(cb, cb, rb, ALU.add)
            dve.tensor_tensor(wgk, wgk, wgv, ALU.add).then_inc(cs_v("gkv"), 1)
            dve.tensor_scalar(cw[:, :, PAD:PAD + 1], cw[:, :, PAD:PAD + 1], 1.0, None, ALU.add).then_inc(cs_v("tap"), 1)
            dve.wait_ge(*cs_v.at("tap", b0))

            def retained(b, c):
                dve.wait_ge(*re_a.at(f"u{c}", b))
                dve.tensor_tensor_scan(ST[:, c, :], a_dec[:, c:c + 1].to_broadcast([P, T]), ST[:, c, :], 0.0,
                                       ALU.mult, ALU.add).then_inc(re_v(f"scan{c}"), 1)
                dve.wait_ge(*re_a.at(f"cv{c}", b))
                for i, k in enumerate(k for k in range(TAPS) if k != PAD):
                    if i:
                        dve.wait_ge(*re_v.at(f"tap{i - 1}_{c}", b))
                    dve.scalar_tensor_tensor(cv[:, c, :], xT[b.slot][:, c, k:k + T], cw[:, c, k:k + 1], cv[:, c, :],
                                             ALU.mult, ALU.add).then_inc(re_v(f"tap{i}_{c}"), 1)

            def norm1_stats(b, tb):
                if tb == 0:
                    dve.wait_ge(*n1_v.at(f"out{TB - 1}", b - 1))
                dve.wait_ge(*n1_a.at(f"raw{tb}", b))
                dve.bn_stats(bn1[:, tb, :], x1[b.slot][:, tb, :]).then_inc(n1_v(f"bn{tb}"), 1)

            def norm1(b):
                dve.wait_ge(*n1_v.at(f"bn{TB - 1}", b))
                hold(dve)
                for tb in range(TB):
                    m = dve.bn_aggr(mv1[:, tb, :], bn1[:, tb, :])
                m.then_inc(n1_v("aggr"), 1)

            def norm1_out(b):
                dve.wait_ge(*n1_p.at("rstd", b))
                for tb in range(TB):
                    dve.tensor_scalar(x1[b.slot][:, tb, :], x1[b.slot][:, tb, :], mv1[:, tb, 0:1], rs1[:, tb:tb + 1],
                                      ALU.subtract, ALU.mult).then_inc(n1_v(f"out{tb}"), 1)

            def weigh(b, h):
                dve.wait_ge(*at_p.at(f"mask{h}", b))
                for i, (at, n) in enumerate(((0, 512), (512, 384), (896, 384))):
                    dve.wait_ge(*at_t.at(f"s{h}_{i}", b))
                    d = Dm[h % ND][:, at:at + n]
                    dve.scalar_tensor_tensor(d, Sb[(3 * h + i) % 2][:, 0:n], DH ** -0.5, d, ALU.mult, ALU.mult)\
                        .then_inc(at_v(f"mul{h}_{i}"), 1)

            def head_out(b, h):
                pv = Pb[h % 2][:, 0:TB * PVN].rearrange("p (a w) -> p a w", a=TB)
                dve.wait_ge(*pv_t.at(f"pv{h}", b))
                if h == 0:
                    dve.wait_ge(*ga_a.at("en", b))
                    dve.wait_ge(*ro_t.at(f"x{TB - 1}", b - 1))
                    dve.wait_ge(*ro_v.at("stats", b - 1))
                    if b.off >= 1:
                        dve.wait_ge(st_x2, b.line(16))
                        dve.wait_ge(st_acc, b.line(16))
                if h:
                    dve.wait_ge(*ev_v.at(f"out{h - 1}", b))
                else:
                    dve.wait_ge(*ev_v.at(f"out{NH - 1}", b - 1))
                dve.scalar_tensor_tensor(den, pv[:, :, DH], -1.0, en[b.slot][:, :, h], ALU.mult, ALU.max)\
                    .then_inc(ev_v(f"neg{h}"), 1)
                dve.wait_ge(*ev_v.at(f"neg{h}", b))
                dve.tensor_tensor(den, pv[:, :, DH], den, ALU.max).then_inc(ev_v(f"den{h}"), 1)
                dve.wait_ge(*ev_v.at(f"den{h}", b))
                dve.tensor_scalar(den, den, CELL_EPS, None, ALU.add).then_inc(ev_v(f"eps{h}"), 1)
                dve.wait_ge(*ev_v.at(f"eps{h}", b))
                dve.reciprocal(den, den).then_inc(ev_v(f"rec{h}"), 1)
                dve.wait_ge(*ev_v.at(f"rec{h}", b))
                dve.tensor_tensor(x2[:, :, h * DH:(h + 1) * DH], pv[:, :, 0:DH],
                                  den.unsqueeze(2).to_broadcast([P, TB, DH]), ALU.mult).then_inc(ev_v(f"out{h}"), 1)

            def norm23(b):
                dve.wait_ge(*l2_v.at(f"out{TB - 1}", b - 1))
                dve.wait_ge(*ev_v.at(f"out{NH - 1}", b))
                for tb in range(TB):
                    m = dve.bn_stats(bn2[:, tb, :], x2[:, tb, :])
                m.then_inc(l2_v("bn2"), 1)
                dve.wait_ge(*l2_v.at("bn2", b))
                hold(dve)
                for tb in range(TB):
                    m = dve.bn_aggr(mv2[:, tb, :], bn2[:, tb, :])
                m.then_inc(l2_v("aggr2"), 1)
                dve.wait_ge(*l2_v.at("aggr2", b))
                for tb in range(TB):
                    m = dve.scalar_tensor_tensor(x2[:, tb, :], x2[:, tb, :], mv2[:, tb, 0:1], lns, ALU.subtract, ALU.mult)
                m.then_inc(l2_v("scaled"), 1)
                dve.wait_ge(*l2_v.at("scaled", b))
                dve.wait_ge(*l2_p.at("rstd2", b))
                for tb in range(TB):
                    m = dve.scalar_tensor_tensor(x2[:, tb, :], x2[:, tb, :], rs2[:, tb:tb + 1], x1[b.slot][:, tb, :],
                                                 ALU.mult, ALU.add)
                m.then_inc(l2_v("sum"), 1)
                dve.wait_ge(*l2_v.at("sum", b))
                for tb in range(TB):
                    m = dve.bn_stats(bn3[:, tb, :], x2[:, tb, :])
                m.then_inc(l2_v("bn3"), 1)
                dve.wait_ge(*l2_v.at("bn3", b))
                hold(dve)
                for tb in range(TB):
                    m = dve.bn_aggr(mv3[:, tb, :], bn3[:, tb, :])
                m.then_inc(l2_v("aggr3"), 1)
                dve.wait_ge(*l2_p.at("rstd3", b))
                for tb in range(TB):
                    dve.tensor_scalar(x2[:, tb, :], x2[:, tb, :], mv3[:, tb, 0:1], rs3[:, tb:tb + 1],
                                      ALU.subtract, ALU.mult).then_inc(l2_v(f"out{tb}"), 1)

            def gates_1(b):
                dve.wait_ge(*ga_a.at("fx", b))
                dve.scalar_tensor_tensor(g_ab[0:NH], g_fx[0:NH], -1.0, g_fx[0:NH], ALU.mult, ALU.max).then_inc(ga_v("abs"), 1)
                dve.tensor_scalar(g_mn[0:NH], g_fx[0:NH], 0.0, None, ALU.min).then_inc(ga_v("min"), 1)

            def gates_2(b):
                dve.wait_ge(*ga_a.at("log", b))
                dve.wait_ge(*ga_v.at("min", b))
                dve.tensor_tensor(g_lf[0:NH], g_mn[0:NH], g_l[0:NH], ALU.subtract).then_inc(ga_v("logf"), 1)
                dve.wait_ge(*ga_v.at("logf", b))
                dve.tensor_tensor_scan(g_cs[0:NH], ones[0:NH].to_broadcast([NH, T]), g_lf[0:NH], 0.0,
                                       ALU.mult, ALU.add).then_inc(ga_v("cum"), 1)
                dve.wait_ge(*ga_v.at("cum", b))
                dve.wait_ge(*ga_t.at("cols", b - 1))
                dve.tensor_tensor(gm[0:NH], g_ig[0:NH], g_cs[0:NH], ALU.subtract).then_inc(ga_v("g"), 1)
                dve.wait_ge(*ga_v.at("g", b))
                dve.tensor_tensor_scan(g_m[0:NH], gm[0:NH], gm[0:NH], -3.0e38, ALU.max, ALU.max).then_inc(ga_v("max"), 1)
                dve.wait_ge(*ga_v.at("max", b))
                dve.scalar_tensor_tensor(gm[32:GATE], g_cs[0:NH], -1.0, g_m[0:NH], ALU.mult, ALU.subtract)\
                    .then_inc(ga_v("neg"), 1)

            def gates_3(b):
                dve.wait_ge(*ga_a.at("hi", b))
                dve.scalar_tensor_tensor(g_r[0:NH], g_m[0:NH], -1.0, bfs[b.slot][0:NH], ALU.mult, ALU.subtract)\
                    .then_inc(ga_v("r1"), 1)

            def gates_4(b):
                dve.wait_ge(*ga_a.at("m0", b))
                dve.tensor_tensor(bfs[b.slot][64:64 + NH], g_r[0:NH], g_m0[0:NH], ALU.subtract).then_inc(ga_v("lo"), 1)

            def router_stats(b, part):
                if part == 0:
                    dve.wait_ge(*l2_v.at(f"out{TB - 1}", b))
                    dve.wait_ge(*ro_t.at("st", b - 1))
                    for tb in range(TB):
                        m = dve.bn_stats(bnr[:, tb, :], x2[:, tb, :])
                    m.then_inc(ro_v("bn"), 1)
                    dve.wait_ge(*ro_v.at("bn", b))
                    hold(dve)
                    for tb in range(TB):
                        m = dve.bn_aggr(mvr[:, tb, :], bnr[:, tb, :])
                    m.then_inc(ro_v("aggr"), 1)
                if part == 1:
                    dve.wait_ge(*ro_v.at("aggr", b))
                    dve.tensor_tensor(vr[:, 1, :], mvr[:, :, 0], mvr[:, :, 0], ALU.mult).then_inc(ro_v("sq"), 1)
                    dve.wait_ge(*ro_v.at("sq", b))
                    dve.tensor_tensor(vr[:, 1, :], vr[:, 1, :], mvr[:, :, 1], ALU.add).then_inc(ro_v("sum"), 1)
                    dve.wait_ge(*ro_v.at("sum", b))
                    dve.tensor_scalar(vr[:, 1, :], vr[:, 1, :], float(D), None, ALU.mult)
                    dve.tensor_scalar(vr[:, 0, :], mvr[:, :, 1], D / (D - 1.0), None, ALU.mult).then_inc(ro_v("vars"), 1)
                    dve.tensor_reduce(st6[:, :, 2], x2, AX.X, ALU.min)
                if part == 2:
                    dve.tensor_reduce(st6[:, :, 3], x2, AX.X, ALU.max)
                if part == 3:
                    dve.wait_ge(st_dum, 64)
                    for tb in range(TB):
                        m = dve.tensor_scalar(junk[:, tb, :], x2[:, tb, :], -SPARSE, None, ALU.is_gt)
                    m.then_inc(ro_v("above"), 1)
                    dve.wait_ge(*ro_v.at("above", b))
                    for tb in range(TB):
                        m = dve.scalar_tensor_tensor(junk[:, tb, :], x2[:, tb, :], SPARSE, junk[:, tb, :], ALU.is_lt,
                                                     ALU.mult, accum_out=nz[:, tb:tb + 1])
                    m.then_inc(ro_v("cnt"), 1)
                    dve.wait_ge(*ro_v.at("cnt", b))
                    dve.tensor_scalar(st6[:, :, 5], nz, 1.0 / D, None, ALU.mult)
                    dve.tensor_copy(st6[:, :, 0], mvr[:, :, 0])
                    dve.wait_ge(*ro_p.at("l2", b))
                    dve.tensor_copy(st6[:, :, 1], vr[:, 0, :])
                    dve.tensor_copy(st6[:, :, 4], vr[:, 1, :]).then_inc(ro_v("stats"), 1)

            def softmax_1(b):
                dve.wait_ge(*ro_a.at("lg", b))
                dve.wait_ge(*ro_v.at("save", b - 1))
                dve.tensor_reduce(nmx, lg, AX.X, ALU.max).then_inc(ro_v("lmax"), 1)
                dve.wait_ge(*ro_v.at("lmax", b))
                dve.tensor_tensor(pr, lg, nmx.unsqueeze(2).to_broadcast([P, TB, NE]), ALU.subtract)\
                    .then_inc(ro_v("lsub"), 1)

            def softmax_2(b):
                dve.wait_ge(*ro_a.at("exp", b))
                dve.tensor_reduce(wsum, pr, AX.X, ALU.add).then_inc(ro_v("lsum"), 1)
                dve.wait_ge(*ro_v.at("lsum", b))
                dve.reciprocal(wsum, wsum).then_inc(ro_v("lrec"), 1)
                dve.wait_ge(*ro_v.at("lrec", b))
                dve.tensor_tensor(pr, pr, wsum.unsqueeze(2).to_broadcast([P, TB, NE]), ALU.mult)\
                    .then_inc(ro_v("prob"), 1)
                dve.wait_ge(*ro_v.at("prob", b))

            def top_two(b):
                hold(dve)
                for tb in range(TB):
                    m = dve.max(top8[:, tb, :], pr[:, tb, :])
                m.then_inc(ro_v("top"), 1)
                dve.wait_ge(*ro_v.at("top", b))
                hold(dve)
                for tb in range(TB):
                    m = dve.max_index(at8[:, tb, :], top8[:, tb, :], pr[:, tb, :])
                m.then_inc(ro_v("at"), 1)
                dve.tensor_tensor(wsum, top8[:, :, 0], top8[:, :, 1], ALU.add).then_inc(ro_v("sum2"), 1)
                dve.wait_ge(*ro_v.at("sum2", b))
                dve.tensor_copy(ex2, at8[:, :, 0:2])
                dve.reciprocal(wsum, wsum).then_inc(ro_v("rec2"), 1)
                dve.wait_ge(*ro_v.at("rec2", b))
                io = iota_e.unsqueeze(1).to_broadcast([P, TB, NE])
                dve.tensor_tensor(oh0, io, ex2[:, :, 0:1].to_broadcast([P, TB, NE]), ALU.is_equal)
                dve.tensor_tensor(oh1, io, ex2[:, :, 1:2].to_broadcast([P, TB, NE]), ALU.is_equal)
                dve.tensor_copy(tiles_of(e_all, b), ex2)
                dve.tensor_tensor(tiles_of(w_all, b), top8[:, :, 0:2], wsum.unsqueeze(2).to_broadcast([P, TB, 2]),
                                  ALU.mult).then_inc(ro_v("oh"), 1)
                dve.wait_ge(*ro_v.at("oh", b))
                dve.tensor_tensor(oh0, oh0, oh1, ALU.add).then_inc(ro_v("ohs"), 1)
                dve.wait_ge(*ro_v.at("ohs", b))
                pair = (b - b.slot).line(NE // 2)
                dve.tensor_tensor(sc_all[:, b.slot * TB:(b.slot + 1) * TB, bass.ds(pair, NE)], oh0, pr, ALU.mult)\
                    .then_inc(ro_v("save"), 1)

            def tiles_of(ap, b):
                return ap.rearrange("p (n a) e -> p n a e", a=TB)[:, b.line(1)]

            def step(n, a, s, r, x1, x2):
                for tb in range(TB):
                    if r:
                        router_stats(n - 2, tb)
                    if a:
                        norm1_stats(n, tb)
                if a:
                    norm1(n)
                    norm1_out(n)
                for h in range(NH):
                    if s:
                        weigh(n - 1, h)
                        if h:
                            head_out(n - 1, h - 1)
                    if h < C and x1:
                        retained(n + 1, h)
                    if r:
                        if h == 0:
                            softmax_1(n - 2)
                        if h == 2:
                            softmax_2(n - 2)
                            top_two(n - 2)
                    if a:
                        if h == 4:
                            gates_1(n)
                        if h == 5:
                            gates_2(n)
                        if h == 6:
                            gates_3(n)
                        if h == 7:
                            gates_4(n)
                if s:
                    head_out(n - 1, NH - 1)
                    norm23(n - 1)

            for c in range(C):
                retained(b0, c)
            run_pipeline(dve, step)

            dve.wait_ge(*ro_v.at("save", bl))
            dve.wait_ge(*se_p.at("iotas", b0))
            for half in range(2):
                dve.wait_ge(*se_t.at(f"scT{half}", b0))
                dve.tensor_copy(scT[:, half * 4:half * 4 + 4, :], Wb[half][:, :].rearrange("p (k t) -> p k t", k=4))\
                    .then_inc(se_v(f"scT{half}"), 1)
            dve.memset(lo, 0).then_inc(se_v("lo"), 1)
            dve.memset(thr, 1 << MAXBIT).then_inc(se_v("thr"), 1)
            dve.wait_ge(*se_v.at("thr", b0))
            thf = thr.bitcast(F32)
            for i in range(NSEL):
                dve.tensor_scalar(cmpb, scT, thf, None, ALU.is_ge, ALU.add, accum_out=cnt).then_inc(se_v(f"cmp{i}"), 1)
                dve.wait_ge(*se_t.at(f"cnt{i}", b0))
                dve.tensor_scalar(bit, Tb[:, 0:1], float(CAP), None, ALU.is_ge).then_inc(se_v(f"bit{i}"), 1)
                dve.wait_ge(*se_v.at(f"bit{i}", b0))
                dve.scalar_tensor_tensor(lo, bit, MAXBIT - i, lo, ALU.logical_shift_left, ALU.bitwise_or)\
                    .then_inc(se_v(f"lo{i}"), 1)
                dve.wait_ge(*se_v.at(f"lo{i}", b0))
                below = 1 << (MAXBIT - i - 1) if i < NSEL - 1 else 0
                dve.tensor_scalar(thr, lo, below, None, ALU.bitwise_or).then_inc(se_v(f"thr{i}"), 1)
                dve.wait_ge(*se_v.at(f"thr{i}", b0))
            dve.tensor_scalar(gt, scT, thf, None, ALU.is_gt, ALU.add, accum_out=cnt).then_inc(se_v("gt"), 1)
            dve.wait_ge(*se_t.at("gtc", b0))
            dve.tensor_scalar(need, Tb[:, 0:1], -1.0, float(CAP), ALU.mult, ALU.add).then_inc(se_v("need"), 1)
            dve.tensor_scalar(off, thf, 0.0, 2.0, ALU.is_equal, ALU.mult).then_inc(se_v("off"), 1)
            dve.wait_ge(*se_v.at("off", b0))
            dve.tensor_tensor(off, off, thf, ALU.add).then_inc(se_v("eqthr"), 1)
            dve.wait_ge(*se_v.at("eqthr", b0))
            dve.tensor_scalar(eq, scT, off, None, ALU.is_equal).then_inc(se_v("eq"), 1)
            dve.wait_ge(*se_v.at("eq", b0))

            def flat(ap):
                return ap.rearrange("p a b -> p (a b)")

            one_row = ones.to_broadcast([P, NT // 4 * P])
            dve.tensor_tensor_scan(flat(cmpb), one_row, flat(eq), 0.0, ALU.mult, ALU.add).then_inc(se_v("eqscan"), 1)
            dve.wait_ge(*se_t.at("eqo", b0))
            dve.tensor_copy(base, Tb[:, 0:1]).then_inc(se_v("eqoff"), 1)
            dve.wait_ge(*se_v.at("eqoff", b0))
            dve.tensor_scalar(cmpb, cmpb, base, need, ALU.add, ALU.is_le).then_inc(se_v("eqok"), 1)
            dve.wait_ge(*se_v.at("eqok", b0))
            dve.tensor_tensor(cmpb, cmpb, eq, ALU.mult).then_inc(se_v("eqsel"), 1)
            dve.wait_ge(*se_v.at("eqsel", b0))
            dve.tensor_tensor(gt, gt, cmpb, ALU.add).then_inc(se_v("sel"), 1)
            dve.wait_ge(*se_v.at("sel", b0))
            dve.tensor_tensor_scan(flat(pos), one_row, flat(gt), 0.0, ALU.mult, ALU.add).then_inc(se_v("scan"), 1)
            dve.wait_ge(*se_t.at("selo", b0))
            dve.tensor_copy(base, Tb[:, 0:1]).then_inc(se_v("selbase"), 1)
            dve.wait_ge(*se_v.at("selbase", b0))
            dve.scalar_tensor_tensor(pos, pos, base, gt, ALU.add, ALU.mult).then_inc(se_v("masked"), 1)
            for half in range(2):
                dve.wait_ge(*se_t.at(f"posT{half}", b0))
                dst = posT.rearrange("p (g k) e -> p k g e", g=4)[:, half * 4:half * 4 + 4]
                dve.tensor_copy(dst, Wb[half][:, :].rearrange("p (k g e) -> p k g e", k=4, g=4))\
                    .then_inc(se_v(f"posT{half}"), 1)
            io = iota_e.unsqueeze(1).to_broadcast([P, NT, NE])
            for k in range(2):
                if k:
                    dve.wait_ge(*se_v.at("s0", b0))
                dve.tensor_tensor(ohk, io, e_all[:, :, k:k + 1].to_broadcast([P, NT, NE]), ALU.is_equal)\
                    .then_inc(se_v(f"oh{k}"), 1)
                dve.wait_ge(*se_v.at(f"oh{k}", b0))
                dve.tensor_tensor(ohk, ohk, posT, ALU.mult).then_inc(se_v(f"pr{k}"), 1)
                dve.wait_ge(*se_v.at(f"pr{k}", b0))
                dve.tensor_reduce(slot[:, k, :], ohk, AX.X, ALU.add).then_inc(se_v(f"s{k}"), 1)
            dve.wait_ge(*se_v.at("s1", b0))
            dve.tensor_scalar(shi, slot, float(P), None, ALU.is_gt).then_inc(se_v("hi"), 1)
            dve.wait_ge(*se_v.at("hi", b0))
            dve.scalar_tensor_tensor(slo, shi, -float(P), slot, ALU.mult, ALU.add).then_inc(se_v("lo_"), 1)
            dve.scalar_tensor_tensor(shi, e_all.rearrange("p t k -> p k t"), 2.0, shi, ALU.mult, ALU.add)\
                .then_inc(se_v("hi2"), 1)
            dve.wait_ge(*se_v.at("hi2", b0))
            for i in range(2 * NT):
                k, tile = i // NT, i % NT
                if i >= 2:
                    dve.wait_ge(*li_t.at(f"m{i - 2}", b0))
                dve.tensor_scalar(Lh[i % 2], iota_l, slo[:, k, tile:tile + 1], None, ALU.is_equal)
                h = shi[:, k, tile:tile + 1]
                dve.tensor_scalar(Hh[i % 2][:, 0, :], iota_h, h, tid[:, tile:tile + 1], ALU.is_equal, ALU.mult)
                dve.tensor_scalar(Hh[i % 2][:, 1, :], iota_h, h, w_all[:, tile, k:k + 1], ALU.is_equal, ALU.mult)\
                    .then_inc(li_v(f"w{i}"), 1)
            dve.wait_ge(*li_t.at(f"m{2 * NT - 1}", b0))
            dve.tensor_copy(tid_l, Tb[:, 0:2 * NE]).then_inc(lf_v("tid"), 1)
            dve.tensor_copy(w_l, Tb[:, 2 * NE:4 * NE]).then_inc(lf_v("w"), 1)
            dve.wait_ge(*lf_v.at("tid", b0))
            dve.tensor_scalar(emp, tid_l, 0.0, None, ALU.is_equal).then_inc(lf_v("empty"), 1)
            dve.wait_ge(*lf_v.at("empty", b0))
            dve.tensor_tensor(emp, emp, iota_s, ALU.mult).then_inc(lf_v("fill"), 1)
            dve.wait_ge(*lf_v.at("fill", b0))
            dve.scalar_tensor_tensor(idx_l, tid_l, -1.0, emp, ALU.add, ALU.add).then_inc(lf_v("idx"), 1)

            def rows_out(e):
                dve.wait_ge(*is_p.at("copy", e - 1))
                w = w_l.rearrange("p (e k) -> p e k", k=2)[:, e.line(1)]
                dve.wait_ge(*yr_t.at("y0", e))
                dve.tensor_scalar(yy[e.slot][:, 0, :], Yb[0][:, :], w[:, 0:1], None, ALU.mult).then_inc(yr_v("y0"), 1)
                dve.wait_ge(*yr_t.at("y1", e))
                dve.tensor_scalar(yy[e.slot][0:CAP2, 1, :], Yb[1][0:CAP2, :], w[0:CAP2, 1:2], None, ALU.mult)\
                    .then_inc(yr_v("y1"), 1)

            def expert(e, first, last):
                for j in range(J + 1):
                    if j == 0:
                        dve.wait_ge(*dn_t.at("d1", e - 1))
                    k = (e.slot * (J + 1) + j) % 2
                    dve.wait_ge(*up_a.at(f"silu{j}", e))
                    u = Ub[k][:, CAP:2 * CAP]
                    if j < J:
                        dve.tensor_tensor(hact[:, j, :], sg[k], u, ALU.mult).then_inc(up_v(f"mul{j}"), 1)
                    else:
                        dve.scalar_tensor_tensor(hact[:, j, :], sg[k], A_SCALE, u, ALU.mult, ALU.mult)\
                            .then_inc(up_v(f"mul{j}"), 1)
                    if j == 1 and not first:
                        rows_out(e - 1)

            run_experts(dve, expert)
            rows_out(Batch(0, NE - 1))

            with dve.Fori(0, (NB) // 2) as i:
                t = i * 2
                for p in range(2):
                    b = Batch(t, p)
                    dve.wait_ge(*fi_v.at("out", b - 1))
                    dve.wait_ge(ld_f[p], b.landed())
                    for tb in range(TB):
                        m = dve.bn_stats(ln_st[:, tb, :], fin[p][:, tb, :])
                    m.then_inc(fi_v("bn"), 1)
                    dve.wait_ge(*fi_v.at("bn", b))
                    hold(dve)
                    for tb in range(TB):
                        m = dve.bn_aggr(ln_mv[:, tb, :], ln_st[:, tb, :])
                    m.then_inc(fi_v("aggr"), 1)
                    dve.wait_ge(*fi_p.at("rstd", b))
                    for tb in range(TB):
                        m = dve.tensor_scalar(fin[p][:, tb, :], fin[p][:, tb, :], ln_mv[:, tb, 0:1], ln_rs[:, tb:tb + 1],
                                              ALU.subtract, ALU.mult)
                    m.then_inc(fi_v("out"), 1)

        @block.gpsimd
        def _(pool):
            start(pool, "pool")
            pool.wait_ge(*cs_v.at("misc", b0))

            def select(ap, pattern, base_, mult, op, fill, done):
                pool.affine_select(out=ap, in_=ap, pattern=pattern, compare_op=op, fill=fill, base=base_,
                                   channel_multiplier=mult).then_inc(done, 1)

            pool.memset(ident, 0.0).then_inc(cs_p("ident0"), 1)
            pool.wait_ge(*cs_p.at("ident0", b0))
            select(ident, [[-1, P]], 0, 1, ALU.not_equal, 1.0, cs_p("ident"))
            pool.memset(sel, 0.0).then_inc(cs_p("sel0"), 1)
            for q in range(3):
                pool.wait_ge(*cs_p.at(f"sel{q}", b0))
                select(sel, [[-1, NH], [0, P]], -32 * q, 1, ALU.not_equal, 1.0, cs_p(f"sel{q + 1}"))
            pool.iota(iota_e, pattern=[[1, NE]], base=0, channel_multiplier=0,
                      allow_small_or_imprecise_dtypes=True).then_inc(cs_p("iota"), 1)

            def power(var, rs, eps, done_eps, wait_eps, done):
                hold(pool)
                pool.tensor_scalar(rs, var, eps, None, ALU.add).then_inc(done_eps, 1)
                pool.wait_ge(*wait_eps)
                pool.tensor_tensor(rs, rs, negh, ALU.pow).then_inc(done, 1)

            def mask(b, h):
                pool.wait_ge(*at_a.at(f"exp{h}", b))
                hold(pool)
                d = Dm[h % ND][:, 0:TB * P].rearrange("p (a s) -> p a s", a=TB)
                m = pool.affine_select(out=d, in_=d, pattern=[[0, TB], [1, P]], compare_op=ALU.is_ge, fill=0.0, base=0,
                                       channel_multiplier=-1)
                m.then_inc(at_p(f"mask{h}"), 1)

            def step(n, a, s, r, x1, x2):
                if s:
                    mask(n - 1, 0)
                if r:
                    pool.wait_ge(*ro_v.at("vars", n - 2))
                    pool.tensor_tensor(vr[:, 0, :], vr[:, 0, :], posh, ALU.pow).then_inc(ro_p("std"), 1)
                    pool.tensor_tensor(vr[:, 1, :], vr[:, 1, :], posh, ALU.pow).then_inc(ro_p("l2"), 1)
                if a:
                    pool.wait_ge(*n1_v.at("aggr", n))
                    power(mv1[:, :, 1], rs1, LN_EPS, n1_p("eps"), n1_p.at("eps", n), n1_p("rstd"))
                for h in range(1, NH):
                    if s:
                        mask(n - 1, h)
                if s:
                    pool.wait_ge(*l2_v.at("aggr2", n - 1))
                    power(mv2[:, :, 1], rs2, LN_EPS, l2_p("eps2"), l2_p.at("eps2", n - 1), l2_p("rstd2"))
                    pool.wait_ge(*l2_v.at("aggr3", n - 1))
                    power(mv3[:, :, 1], rs3, LN_EPS, l2_p("eps3"), l2_p.at("eps3", n - 1), l2_p("rstd3"))

            run_pipeline(pool, step)

            pool.wait_ge(*ro_v.at("save", bl))
            pool.wait_ge(*ro_t.at("lg", bl))
            pool.wait_ge(st_x2, 16 * NB)
            pool.wait_ge(st_acc, 16 * NB)
            pool.memset(blk, 0.0)
            pool.memset(low, 0.0).then_inc(se_p("blk0"), 1)
            for i, d in enumerate((0, -1, 1, -2, 2, -3, 3)):
                pool.wait_ge(*se_p.at(f"blk{i}", b0))
                if d < 0:
                    select(low, [[-1, P]], -32 * d, 1, ALU.not_equal, 1.0, se_p(f"low{-d}"))
                select(blk, [[-1, P]], -32 * d, 1, ALU.not_equal, 1.0, se_p(f"blk{i + 1}"))
            pool.iota(iota_l, pattern=[[1, P]], base=1, channel_multiplier=0, allow_small_or_imprecise_dtypes=True)
            pool.iota(iota_h, pattern=[[1, 2 * NE]], base=0, channel_multiplier=0, allow_small_or_imprecise_dtypes=True)
            pool.iota(tid, pattern=[[P, NT]], base=1, channel_multiplier=1, allow_small_or_imprecise_dtypes=True)
            pool.iota(iota_s.rearrange("p (e k) -> p e k", k=2), pattern=[[0, NE], [P, 2]], base=NTOK + 1,
                      channel_multiplier=1, allow_small_or_imprecise_dtypes=True).then_inc(se_p("iotas"), 1)

            def columns(e, ix, done):
                pool.tensor_copy(ix[e.slot], idx_l.rearrange("p (e k) -> p e k", k=2)[:, e.line(1)]).then_inc(done, 1)

            def gather(e):
                pool.wait_ge(*xr_t.at("x1", e - 2))
                columns(e, idx_g, ig_p("copy"))
                pool.wait_ge(*ig_p.at("copy", e))
                hold(pool)
                for k, n in enumerate((P, CAP2)):
                    pool.indirect_dma_start(out=xg[e.slot][0:n, k, :], out_offset=None, in_=x2_d,
                                            in_offset=bass.IndirectOffsetOnAxis(ap=idx_g[e.slot][0:n, k:k + 1], axis=0))\
                        .then_inc(ld_g[e.slot], 16)

            def scatter(e):
                if e.off:
                    pool.wait_ge(st_y, e.line(32))
                columns(e, idx_s, is_p("copy"))
                pool.wait_ge(*is_p.at("copy", e))
                pool.wait_ge(*yr_v.at("y1", e))
                hold(pool)
                for k, n in enumerate((P, CAP2)):
                    pool.indirect_dma_start(out=acc_d,
                                            out_offset=bass.IndirectOffsetOnAxis(ap=idx_s[e.slot][0:n, k:k + 1], axis=0),
                                            in_=yy[e.slot][0:n, k, :], in_offset=None, compute_op=ALU.add)\
                        .then_inc(st_y, 16)

            pool.wait_ge(*lf_v.at("idx", b0))
            pool.wait_ge(st_dum, 64)
            gather(b0)
            gather(b0 + 1)
            for p in range(2):
                scatter(Batch(0, p))
                gather(Batch(0, 2 + p))
            with pool.Fori(0, (NE - 4) // 2) as i:
                t = i * 2
                for p in range(2):
                    scatter(Batch(t, 2 + p))
                    gather(Batch(t, 4 + p))
            for p in range(2):
                scatter(Batch(0, NE - 2 + p))

            with pool.Fori(0, (NB) // 2) as i:
                t = i * 2
                for p in range(2):
                    b = Batch(t, p)
                    pool.wait_ge(*fi_v.at("aggr", b))
                    power(ln_mv[:, :, 1], ln_rs, LN_EPS, fi_p("eps"), fi_p.at("eps", b), fi_p("rstd"))


def kernel(**inputs):
    import numpy as np
    import concourse.bacc as bacc
    from concourse.bass_utils import run_bass_kernel_spmd

    g = {k.replace("L0_", ""): np.asarray(v) for k, v in inputs.items()}

    def chunks(a):
        a = a.reshape(a.shape[:-2] + (a.shape[-2] // P, P, a.shape[-1]))
        return np.swapaxes(a, -3, -2)

    def column(a):
        return a.reshape(-1, P).T

    arrays = {
        "xT": chunks(np.swapaxes(g["x"], 1, 2)),
        "kT": chunks(np.swapaxes(g["ctx_1024"], 1, 2)),
        "v": np.swapaxes(g["ctx_1024"].reshape(NB, TB, P, NH, DH), 1, 2),
        "decay": column(g["attn_decay_logit"]),
        "WT": chunks(g["attn_W"].T),
        "b": column(g["attn_b"]),
        "cw": np.swapaxes(g["attn_conv_w"].reshape(C, P, TAPS), 0, 1),
        "cb": column(g["attn_conv_b"]),
        "wi": chunks(g["xattn_igate_w"].T),
        "wf": chunks(g["xattn_fgate_w"].T),
        "ib": g["xattn_igate_b"][:, None],
        "fb": g["xattn_fgate_b"][:, None],
        "ln": g["xattn_ln_scale"][None],
        "r1x": chunks(g["ffn_r1_w"][:, :D].T),
        "r1s": g["ffn_r1_w"][:, D:].T,
        "r1b": column(g["ffn_r1_b"]),
        "r2": chunks(g["ffn_r2_w"].T),
        "wup": chunks(np.swapaxes(g["ffn_w_up"], 1, 2)),
        "wdn": chunks(np.swapaxes(g["ffn_w_down"], 1, 2)),
        "aup": chunks(np.swapaxes(g["ffn_a_up"], 1, 2)),
        "adn": np.swapaxes(g["ffn_a_down"], 1, 2),
    }
    nc = bacc.Bacc("TRN2", target_bir_lowering=False, num_devices=1)
    args, feed = [], {}
    for name, a in arrays.items():
        a = np.ascontiguousarray(a)
        feed[f"in_{name}"] = a
        args.append(nc.dram_tensor(f"in_{name}", a.shape, mybir.dt.from_np(a.dtype), kind="ExternalInput").ap())
    out = nc.dram_tensor("out", (NB, T, D), F32, kind="ExternalOutput")
    decoder_kernel(nc, *args, out.ap())
    r = run_bass_kernel_spmd(nc, [feed], core_ids=[0])
    return r.results[0]["out"]
```

```python
from contextlib import ExitStack

import concourse.bass as bass
from concourse import mybir

F32 = mybir.dt.float32
BF16 = mybir.dt.bfloat16
I32 = mybir.dt.int32
U32 = mybir.dt.uint32
ALU = mybir.AluOpType
ACT = mybir.ActivationFunctionType
AX = mybir.AxisListType

P = 128
NB, T, D = 8, 512, 512
C = D // P
TB = T // P
NT = NB * TB
TAPS, PAD = 5, 2
NH, DH = 8, 64
NE, NG = 32, 16
RH = D // 2
RM = RH // P
INTER, AINT = 1024, 128
J = INTER // P
CAP = int(1.25 * NB * T / NE)
CAP2 = CAP - P
NTOK = NB * T
NSTAT = 6
GATE = 40
VW = DH + 1
PVN = 96
LN_EPS, CELL_EPS, SPARSE, A_SCALE = 1e-5, 1e-6, 1e-6, 0.05
AFTER = [512, 896, 1152]
AFTERW = [384, 256, 128]
SCW = 1280
MAXBIT = 29


class Batch:

    def __init__(self, t, off):
        self.t, self.off, self.slot = t, off, off % 2

    def __add__(self, k):
        return Batch(self.t, self.off + k)

    def __sub__(self, k):
        return Batch(self.t, self.off - k)

    def line(self, per, k=0):
        fixed = self.off * per + k
        return fixed if isinstance(self.t, int) else self.t * per + fixed

    def landed(self, dmas=1):
        fixed = 16 * dmas * (self.off // 2 + 1)
        return fixed if isinstance(self.t, int) else self.t * (8 * dmas) + fixed


class Steps:

    def __init__(self, sem, names, lead=0):
        self.sem, self.names, self.lead, self.next = sem, names, lead, 0
        self.index = {n: i for i, n in enumerate(names)}

    def __call__(self, name):
        assert self.names[self.next] == name, (name, self.names[self.next])
        self.next = (self.next + 1) % len(self.names)
        return self.sem

    def at(self, name, b):
        per = len(self.names)
        return self.sem, b.line(per, self.lead * per + self.index[name] + 1)

    def start(self, eng):
        if self.lead:
            eng.sem_inc(self.sem, self.lead * len(self.names))


class Room:

    def __init__(self, arena, size, used=0):
        self.arena, self.size, self.used = arena, size, used

    def take(self, *shape, dt=F32):
        n = 1
        for s in shape:
            n *= s
        words = n if dt != BF16 else (n + 1) // 2
        at, self.used = self.used, self.used + words + words % 2
        assert self.used <= self.size, (self.used, self.size)
        v = self.arena[:, at:at + words]
        if dt != F32:
            v = v.bitcast(dt)
        if len(shape) == 2:
            v = v.rearrange("p (a b) -> p a b", a=shape[0])
        if len(shape) == 3:
            v = v.rearrange("p (a b c) -> p a b c", a=shape[0], b=shape[1])
        return v


def run_pipeline(eng, step):
    full = dict(a=True, s=True, r=True, x1=True, x2=True)
    step(Batch(0, 0), **full | dict(s=False, r=False))
    step(Batch(0, 1), **full | dict(r=False))
    with eng.Fori(0, (NB - 4) // 2) as i:
        t = i * 2
        for p in range(2):
            step(Batch(t, 2 + p), **full)
    step(Batch(0, NB - 2), **full | dict(x2=False))
    step(Batch(0, NB - 1), **full | dict(x1=False, x2=False))
    step(Batch(0, NB), **full | dict(a=False, x1=False, x2=False))
    step(Batch(0, NB + 1), **full | dict(a=False, s=False, x1=False, x2=False))


def run_experts(eng, expert):
    expert(Batch(0, 0), True, False)
    expert(Batch(0, 1), False, False)
    with eng.Fori(0, (NE - 4) // 2) as i:
        t = i * 2
        for p in range(2):
            expert(Batch(t, 2 + p), False, False)
    expert(Batch(0, NE - 2), False, False)
    expert(Batch(0, NE - 1), False, True)


def decoder_kernel(nc, xT_d, kT_d, v_d, decay_d, WT_d, b_d, cw_d, cb_d, wi_d, wf_d, ib_d, fb_d, ln_d,
                   r1x_d, r1s_d, r1b_d, r2_d, wup_d, wdn_d, aup_d, adn_d, out_d):
    x2_d = nc.dram_tensor("x2_rows", (NTOK + CAP, D), F32, kind="Internal").ap()
    acc_d = nc.dram_tensor("acc_rows", (NTOK + CAP, D), F32, kind="Internal").ap()
    ctx = ExitStack()
    with ctx:
        def sem(name):
            return ctx.enter_context(nc.semaphore(name))

        every = {e: [] for e in ("tensor", "vector", "scalar", "pool")}

        def steps(name, names, lead=3):
            p = Steps(sem(name), names, lead)
            every[name.split("_")[-1]].append(p)
            return p

        held = sem("held")

        def hold(eng):
            eng.sem_inc(held, 1)

        def start(eng, name):
            for p in every[name]:
                p.start(eng)

        ROOM = 51520
        arena = ctx.enter_context(nc.sbuf_tensor("arena", [P, ROOM], F32))
        keep_t = ctx.enter_context(nc.sbuf_tensor("keep", [P, 1684], F32))
        bank = [ctx.enter_context(nc.psum_tensor(f"bank{i}", [P, 512], F32)) for i in range(8)]

        keep = Room(keep_t, 1684)
        ident = keep.take(P)
        ones = keep.take(1)
        negh = keep.take(TB)
        posh = keep.take(TB)
        sc_all = keep.take(NT // 4, 4 * NE)
        w_all = keep.take(NT, 2)
        e_all = keep.take(NT, 2)
        tid_l = keep.take(2 * NE)
        w_l = keep.take(2 * NE)
        idx_l = keep.take(2 * NE, dt=I32)
        iota_e = keep.take(NE)
        idx_g = [keep.take(2, dt=I32) for _ in range(2)]
        idx_s = [keep.take(2, dt=I32) for _ in range(2)]

        room = Room(arena, ROOM)
        WT = room.take(C, D)
        wgq = room.take(C, GATE)
        wgk = room.take(C, GATE)
        gbias = room.take(1)
        a_dec = room.take(C)
        a_one = room.take(C)
        cw = room.take(C, TAPS)
        cb = room.take(C)
        rb = room.take(C)
        lns = room.take(D)
        r1x = room.take(C, RH)
        r1s = room.take(RH)
        r1b = room.take(RM)
        r2 = room.take(RM, NE)
        sel = room.take(NH, P, dt=BF16)
        xT = room.take(C, T + 2 * PAD)
        ST = room.take(C, T)
        cv = room.take(C, T)
        x1 = [room.take(TB, D) for _ in range(2)]
        qT = [room.take(C, T) for _ in range(2)]
        kT = room.take(C, T)
        kz = [room.take(2, C, T) for _ in range(2)]
        va = [room.take(TB, NH * VW + PVN - VW) for _ in range(2)]
        ND = 3
        Dm = [room.take(SCW) for _ in range(ND)]
        x2 = [room.take(TB, D) for _ in range(2)]
        x2T = room.take(C, T)
        hg = room.take(RM, T)
        wgv = hg[:, 0, 0:C * GATE].rearrange("p (c g) -> p c g", c=C)
        stT = room.take(T)
        zeros = room.take(2 * D)
        g_fx, g_ab, g_mn, g_ig = (room.take(T) for _ in range(4))
        g_l = g_ab
        g_lf = g_mn
        g_cs = g_fx
        g_m = room.take(T)
        g_r = g_mn
        g_m0 = room.take(T, dt=BF16)
        gm = room.take(T)
        bfs = [room.take(T, dt=BF16) for _ in range(2)]
        gcol = [room.take(TB, GATE) for _ in range(2)]
        ng = [room.take(TB, NH) for _ in range(2)]
        en = [room.take(TB, NH) for _ in range(2)]
        bn1 = room.take(TB, 6)
        mv1 = room.take(TB, 2)
        rs1 = room.take(TB)
        den = room.take(TB)
        nz = room.take(TB)
        bn2 = room.take(TB, 6)
        mv2 = room.take(TB, 2)
        rs2 = room.take(TB)
        bn3 = room.take(TB, 6)
        mv3 = room.take(TB, 2)
        rs3 = room.take(TB)
        bnr = room.take(TB, 6)
        mvr = room.take(TB, 2)
        vr = room.take(2, TB)
        st6 = room.take(TB, NSTAT)
        junk = zeros.bitcast(BF16).rearrange("p (a d) -> p a d", a=TB)
        zeros = zeros[:, 0:D]
        lg = room.take(TB, NE)
        nmx = room.take(TB)
        pr = room.take(TB, NE)
        top8 = room.take(TB, 8)
        at8 = room.take(TB, 8, dt=U32)
        ex2 = room.take(TB, 2)
        oh0 = room.take(TB, NE)
        oh1 = room.take(TB, NE)
        wsum = room.take(TB)

        Wb = bank[0:2]
        Tb = bank[2]
        Sb = bank[3:5]
        Bb = bank[5]
        Pb = bank[6:8]

        ld_first = sem("ld_first_consts")
        ld_c = sem("ld_consts")
        ld_x = sem("ld_x")
        ld_k = sem("ld_k")
        ld_z = [sem(f"ld_kz{i}") for i in range(2)]
        ld_v = [sem(f"ld_v{i}") for i in range(2)]
        st_x2 = [sem(f"st_x2_{i}") for i in range(2)]
        st_acc = [sem(f"st_acc{i}") for i in range(2)]
        st_dum = sem("st_dummy_rows")

        cs_v = steps("const_vector", ["misc", "dec1", "dec2", "tap", "gkv"], 0)
        cs_a = steps("const_scalar", ["dec"], 0)
        cs_p = steps("const_pool", ["ident0", "ident"] + [f"sel{q}" for q in range(4)] + ["iota", "kz"], 0)
        re_a = steps("ret_scalar", [x for c in range(C) for x in (f"u{c}", f"cv{c}")])
        re_v = steps("ret_vector", [x for c in range(C) for x in
                                    [f"scan{c}"] + [f"tap{k}_{c}" for k in range(TAPS - 1)]])
        re_t = steps("ret_tensor", [f"w{tb}" for tb in range(TB)])
        n1_a = steps("ln1_scalar", [f"raw{tb}" for tb in range(TB)])
        n1_v = steps("ln1_vector", [f"bn{tb}" for tb in range(TB)] + ["aggr"] + [f"out{tb}" for tb in range(TB)])
        n1_p = steps("ln1_pool", ["eps", "rstd"])
        qt_t = steps("qT_tensor", [f"t{tb}" for tb in range(TB)])
        qt_a = steps("qT_scalar", [f"q{tb}" for tb in range(TB)])
        ga_t = steps("gate_tensor", ["gates_k", "gates", "cols"])
        ga_a = steps("gate_scalar", ["ig", "fx", "exp", "log", "hi", "m0", "mid", "gcol", "ng", "en"])
        ga_v = steps("gate_vector", ["abs", "min", "logf", "cum", "g", "max", "neg", "r1", "lo"])
        bc_t = steps("max_tensor", [f"bc{h}" for h in range(NH)])
        at_t = steps("att_tensor", [f"s{h}_{i}" for h in range(NH) for i in range(3)])
        pv_t = steps("pv_tensor", [f"pv{h}" for h in range(NH)])
        at_a = steps("att_scalar", [x for h in range(NH) for x in (f"relu{h}", f"exp{h}")])
        at_p = steps("att_pool", [f"mask{h}" for h in range(NH)])
        at_v = steps("att_vector", [f"mul{h}_{i}" for h in range(NH) for i in range(3)])
        ev_v = steps("ev_vector", [x for h in range(NH) for x in (f"neg{h}", f"den{h}", f"eps{h}", f"rec{h}", f"out{h}")])
        l2_v = steps("ln2_vector", ["bn2", "aggr2", "scaled", "sum", "bn3", "aggr3"] +
                     [f"out{tb}" for tb in range(TB)])
        l2_p = steps("ln2_pool", ["eps2", "rstd2", "eps3", "rstd3"])
        ro_t = steps("router_tensor", [f"x{tb}" for tb in range(TB)] + ["st", "h0", "h1", "lg"])
        ro_a = steps("router_scalar", [f"x{tb}" for tb in range(TB)] + ["st", "h0", "h1", "lg", "exp"])
        ro_v = steps("router_vector", ["bn", "aggr", "sq", "sum", "vars", "above", "cnt", "stats",
                                       "lmax", "lsub", "lsum", "lrec", "prob", "top", "at",
                                       "sum2", "rec2", "oh", "ohs", "save"])
        ro_p = steps("router_pool", ["std", "l2"])
        b0 = Batch(0, 0)
        bl = Batch(0, NB - 1)

        xc = xT[:, :, PAD:PAD + T]

        room2 = Room(arena, ROOM)
        wu = [room2.take(C, 2 * INTER) for _ in range(2)]
        wd = [room2.take(J, D) for _ in range(2)]
        au = [room2.take(C, 2 * AINT) for _ in range(2)]
        ad = [room2.take(D) for _ in range(2)]
        late = room2.used
        scT = room2.take(NT // 4, P)
        cmpb = room2.take(NT // 4, P)
        scH = room2.take(NT // 4 * P, dt=BF16)
        cmpH = room2.take(NT // 4 * P, dt=BF16)
        thr = room2.take(1, dt=I32)
        bit = room2.take(1, dt=I32)
        cnt = room2.take(1)
        need = room2.take(1)
        gt = room2.take(NT // 4, P)
        eq = room2.take(NT // 4, P)
        pos = room2.take(NT // 4, P)
        base = room2.take(1)
        blk = room2.take(P)
        low = room2.take(P)
        posT = room2.take(NT, NE)
        ohk = room2.take(NT, NE)
        emp = room2.take(2 * NE)
        off = room2.take(1)
        slot = room2.take(2, NT)
        shi = room2.take(2, NT)
        slo = room2.take(2, NT)
        tid = room2.take(NT)
        iota_h = room2.take(2 * NE)
        iota_l = room2.take(P)
        iota_s = room2.take(2 * NE)
        LG = 8
        Lh = [room2.take(LG, P) for _ in range(2)]
        Hh = [room2.take(LG, 2, 2 * NE) for _ in range(2)]
        room3 = Room(arena, ROOM, late)
        xg = [room3.take(2, D) for _ in range(2)]
        xeT = room3.take(C, CAP)
        sg = [room3.take(CAP) for _ in range(2)]
        hact = room3.take(J + 1, CAP)
        yT = room3.take(C, CAP)
        yy = [room3.take(2, D) for _ in range(2)]
        room4 = Room(arena, ROOM)
        fin = [room4.take(TB, D) for _ in range(NB)]
        ln_st = [room4.take(TB, 6) for _ in range(2)]
        ln_mv = [room4.take(TB, 2) for _ in range(2)]
        ln_rs = [room4.take(TB) for _ in range(2)]

        Ub = bank[0:2]
        Db = bank[2:4]
        Xb = bank[4:6]
        Yb = bank[6:8]

        ld_wu = [sem(f"ld_wup{i}") for i in range(2)]
        ld_wd = [sem(f"ld_wdown{i}") for i in range(2)]
        ld_au = [sem(f"ld_aup{i}") for i in range(2)]
        ld_ad = [sem(f"ld_adown{i}") for i in range(2)]
        ld_g = [sem(f"gathered{i}") for i in range(2)]
        st_y = sem("scattered")
        NSEL = MAXBIT + 1
        se_v = steps("sel_vector", ["scT0", "scT1", "thr", "upper"] +
                     [x for i in range(NSEL) for x in (f"cmp{i}", f"bit{i}", f"thr{i}")] +
                     ["gt", "need", "off", "eqthr", "eq", "eqscan", "eqoff", "eqok", "eqsel", "sel", "scan",
                      "selbase", "masked", "posT0", "posT1", "oh0", "pr0", "s0", "oh1", "pr1", "s1",
                      "hi", "lo_", "hi2"], 0)
        se_p = steps("sel_pool", ["blk0", "blk1", "low1", "blk2", "blk3", "low2", "blk4", "blk5", "low3", "blk6",
                                  "blk7", "iotas"], 0)
        se_t = steps("sel_tensor", ["scT0", "scT1"] + [f"cnt{i}" for i in range(NSEL)] +
                     ["gtc", "eqo", "selo", "posT0", "posT1"], 0)
        li_v = steps("list_vector", [f"{x}{i}" for i in range(2 * NT // LG) for x in ("oh", "w", "t")], 0)
        li_t = steps("list_tensor", [f"m{i}" for i in range(2 * NT // LG)], 0)
        lf_v = steps("listfin_vector", ["tid", "w", "empty", "fill", "idx"], 0)
        up_t = steps("up_tensor", [f"up{j}" for j in range(J + 1)], 2)
        up_a = steps("up_scalar", [f"silu{j}" for j in range(J + 1)], 2)
        up_v = steps("up_vector", [f"mul{j}" for j in range(J + 1)], 2)
        xr_t = steps("rowsin_tensor", ["x0", "x1"], 2)
        xr_a = steps("rowsin_scalar", ["x0", "x1"], 2)
        dn_t = steps("down_tensor", ["d0", "d1"], 2)
        dn_a = steps("down_scalar", ["d0", "d1"], 2)
        yr_t = steps("rowsout_tensor", ["y0", "y1"], 2)
        yr_v = steps("rowsout_vector", ["y0", "y1"], 2)
        ig_p = steps("gatherindex_pool", ["copy"])
        is_p = steps("scatterindex_pool", ["copy"])
        ld_f = [sem(f"ld_fin{i}") for i in range(NB)]
        st_f = sem("st_fin")
        fb_v = steps("finstats_vector", ["bn", "aggr"], 2)
        fi_v = steps("fin_vector", ["out"], 2)
        fi_p = steps("fin_pool", ["eps", "rstd"], 2)

        NCONST = 14
        block = ctx.enter_context(nc.Block())

        @block.sync
        def _(sp):
            for done in st_x2 + st_acc:
                sp.sem_inc(done, 16)
            def load_x(b):
                sp.wait_ge(*re_v.at(f"tap{TAPS - 2}_{C - 1}", b - 1))
                sp.dma_start(xc, xT_d[b.line(1)]).then_inc(ld_x, 16)

            def load_context(b):
                sp.wait_ge(*ga_t.at("gates_k", b - 1))
                sp.dma_start(kT, kT_d[b.line(1)]).then_inc(ld_k, 16)
                sp.wait_ge(*pv_t.at(f"pv{NH - 1}", b - 2))
                for r in range(2):
                    half = slice(r * DH, (r + 1) * DH)
                    sp.dma_start(kz[b.slot][half, r], kT_d[b.line(1), half]).then_inc(ld_z[b.slot], 16)
                for tb in range(TB):
                    dst = va[b.slot][:, tb, 0:NH * VW].rearrange("p (h w) -> p h w", h=NH)[:, :, 0:DH]
                    sp.dma_start(dst, v_d[b.line(1), :, tb]).then_inc(ld_v[b.slot], 16)

            def store_x2(b):
                sp.wait_ge(*l2_v.at(f"out{TB - 1}", b))
                for rows, done in ((x2_d, st_x2), (acc_d, st_acc)):
                    dst = rows[0:NTOK].rearrange("(n a p) d -> n p a d", a=TB, p=P)[b.line(1)]
                    sp.dma_start(dst, x2[b.slot]).then_inc(done[b.slot], 16)

            def step(n, a, s, r, x1, x2):
                if a:
                    load_context(n)
                if r:
                    store_x2(n - 2)
                if x2:
                    load_x(n + 2)

            for dst, src in ((a_dec, decay_d), (cw, cw_d), (cb, cb_d), (rb, b_d)):
                sp.dma_start(dst, src).then_inc(ld_first, 16)
            load_x(b0)
            sp.dma_start(WT, WT_d).then_inc(ld_c, 16)
            sp.wait_ge(*cs_v.at("misc", b0))
            for dst, src in ((wgq[:, :, 0:NH], wi_d[:, 0:C]), (wgk[:, :, 0:NH], wi_d[:, C:2 * C]),
                             (wgv[:, :, 0:NH], wi_d[:, 2 * C:]), (wgq[:, :, 32:GATE], wf_d[:, 0:C]),
                             (wgk[:, :, 32:GATE], wf_d[:, C:2 * C]), (wgv[:, :, 32:GATE], wf_d[:, 2 * C:]),
                             (gbias[0:NH], ib_d), (gbias[32:GATE], fb_d), (lns, ln_d.to_broadcast([P, D])),
                             (r1x, r1x_d), (r1s[0:NSTAT], r1s_d), (r1b, r1b_d), (r2, r2_d)):
                sp.dma_start(dst, src).then_inc(ld_c, 16)
            for rows in (x2_d, acc_d):
                sp.dma_start(rows[NTOK:NTOK + P], zeros).then_inc(st_dum, 16)
                sp.dma_start(rows[NTOK + P:], zeros[0:CAP2]).then_inc(st_dum, 16)
            load_x(b0 + 1)
            sp.wait_ge(*cs_p.at("kz", b0))
            run_pipeline(sp, step)

            sp.wait_ge(*ro_v.at("save", bl))
            sp.wait_ge(*ro_t.at("lg", bl))
            for done in st_x2 + st_acc:
                sp.wait_ge(done, 16 * NB // 2 + 16)

            def load_expert(e, pair):
                s = e.slot
                sp.wait_ge(*up_t.at(f"up{J - 1}", e - 2))
                sp.dma_start(wu[s], wup_d[e.line(1)]).then_inc(ld_wu[s], 16)
                sp.wait_ge(*up_t.at(f"up{J}", e - 2))
                sp.dma_start(au[s], aup_d[pair]).then_inc(ld_au[s], 16)
                sp.wait_ge(*dn_t.at("d1", e - 2))
                sp.dma_start(wd[s], wdn_d[e.line(1)]).then_inc(ld_wd[s], 16)
                sp.dma_start(ad[s], adn_d[pair]).then_inc(ld_ad[s], 16)

            for p in range(2):
                load_expert(Batch(0, p), 0)
            with sp.Fori(0, NE // 2 - 1) as i:
                t, pair = i * 2, i + 1
                for p in range(2):
                    load_expert(Batch(t, 2 + p), pair)

            sp.wait_ge(st_y, 32 * NE)
            for b in range(NB):
                src = acc_d[0:NTOK].rearrange("(n a p) d -> n p a d", a=TB, p=P)[b]
                sp.dma_start(fin[b], src).then_inc(ld_f[b], 16)
            for b in range(NB):
                sp.wait_ge(*fi_v.at("out", Batch(0, b)))
                sp.dma_start(out_d[b].rearrange("(a p) d -> p a d", p=P), fin[b]).then_inc(st_f, 16)
            sp.wait_ge(st_f, 16 * NB)

        @block.tensor
        def _(pe):
            start(pe, "tensor")
            pe.wait_ge(ld_c, 16 * NCONST)
            pe.wait_ge(*cs_p.at("kz", b0))
            pe.wait_ge(*cs_v.at("gkv", b0))

            def broadcast_max(b, h):
                if h == 0:
                    pe.wait_ge(*ga_v.at("lo", b))
                    pe.wait_ge(*ga_a.at("mid", b))
                    pe.wait_ge(*at_a.at(f"exp{NH - 1}", b - 1))
                else:
                    pe.wait_ge(*at_a.at(f"exp{h - 1}", b))
                pe.matmul(Bb[:, :], sel[:, h, :], bfs[b.slot], start=True, stop=True).then_inc(bc_t(f"bc{h}"), 1)

            def retention(b, tb):
                pe.wait_ge(*re_v.at(f"tap{TAPS - 2}_{C - 1}", b))
                w = Wb[tb % 2]
                if tb < 2:
                    pe.wait_ge(*qt_a.at(f"q{tb + 2}", b - 1))
                    pe.wait_ge(*ro_a.at(f"h{tb}", b - 3))
                else:
                    pe.wait_ge(*n1_a.at(f"raw{tb - 2}", b))
                rows = slice(tb * P, (tb + 1) * P)
                for c in range(C):
                    pe.matmul(w[:, :], ST[:, c, rows], WT[:, c, :], start=(c == 0), stop=False)
                for c in range(C):
                    m = pe.matmul(w[:, c * P:(c + 1) * P], cv[:, c, rows], ident, start=False, stop=(c == C - 1))
                m.then_inc(re_t(f"w{tb}"), 1)

            def queries(b):
                for tb in range(TB):
                    w = Wb[tb % 2]
                    pe.wait_ge(*n1_v.at(f"out{tb}", b))
                    if tb >= 2:
                        pe.wait_ge(*qt_a.at(f"q{tb - 2}", b))
                    else:
                        pe.wait_ge(*ro_a.at(f"x{tb + 2}", b - 2))
                    for c in range(C):
                        m = pe.transpose(w[:, c * P:(c + 1) * P], x1[b.slot][:, tb, c * P:(c + 1) * P], ident)
                    m.then_inc(qt_t(f"t{tb}"), 1)

            def gates_k(b):
                pe.wait_ge(ld_k, b.line(16, 16))
                pe.wait_ge(*ga_a.at("gcol", b - 1))
                pe.wait_ge(*ro_a.at("lg", b - 3))
                for c in range(C):
                    m = pe.matmul(Tb[0:GATE, :], wgk[:, c, :], kT[:, c, :], start=(c == 0), stop=False)
                m.then_inc(ga_t("gates_k"), 1)

            def gates_q(b):
                pe.wait_ge(*qt_a.at(f"q{TB - 1}", b))
                for c in range(C):
                    m = pe.matmul(Tb[0:GATE, :], wgq[:, c, :], qT[b.slot][:, c, :], start=False, stop=(c == C - 1))
                m.then_inc(ga_t("gates"), 1)

            def gate_columns(b):
                pe.wait_ge(*ga_v.at("neg", b))
                pe.wait_ge(*ro_a.at("lg", b - 2))
                hold(pe)
                for tb in range(TB):
                    m = pe.transpose(Tb[:, tb * GATE:(tb + 1) * GATE], gm[0:GATE, tb * P:(tb + 1) * P],
                                     ident[0:GATE, 0:GATE])
                m.then_inc(ga_t("cols"), 1)

            def scores(b, h, chunks):
                if (h, chunks[0]) == (0, 0):
                    pe.wait_ge(ld_z[b.slot], b.landed(2))
                own = [(tb * P, P, tb, tb) for tb in range(TB)]
                rest = [(AFTER[tb] - AFTER[min(tb, 1)], AFTERW[tb], tb, tb + 1) for tb in range(TB - 1)]
                for i in chunks:
                    parts = (own, rest[:1], rest[1:])[i]
                    k = 3 * h + i
                    if k >= 2:
                        pe.wait_ge(*at_v.at(f"mul{(k - 2) // 3}_{(k - 2) % 3}", b))
                    else:
                        pe.wait_ge(*at_v.at(f"mul{NH - 1}_{1 + k}", b - 1))
                    for at, n, tb, q in parts:
                        m = pe.matmul(Sb[k % 2][:, at:at + n], kz[b.slot][:, h % 2, h // 2, tb * P:(tb + 1) * P],
                                      qT[b.slot][:, h // 2, q * P:q * P + n], start=True, stop=True)
                    m.then_inc(at_t(f"s{h}_{i}"), 1)

            def values(b, h):
                if h == 0:
                    pe.wait_ge(ld_v[b.slot], b.landed(TB))
                pe.wait_ge(*at_v.at(f"mul{h}_2", b))
                if h >= 2:
                    pe.wait_ge(*ev_v.at(f"out{h - 2}", b))
                else:
                    pe.wait_ge(*ev_v.at(f"out{NH - 2 + h}", b - 1))
                for sb in range(TB):
                    for tb in range(sb + 1):
                        at = tb * P if sb == tb else AFTER[tb] + (sb - tb - 1) * P
                        m = pe.matmul(Pb[h % 2][:, sb * PVN:(sb + 1) * PVN], Dm[h % ND][:, at:at + P],
                                      va[b.slot][:, tb, h * VW:h * VW + PVN], start=(tb == 0), stop=(tb == sb))
                m.then_inc(pv_t(f"pv{h}"), 1)

            def router_in(b, before):
                for tb in range(TB):
                    w = Wb[tb % 2]
                    pe.wait_ge(*l2_v.at(f"out{tb}", b))
                    if tb >= 2:
                        pe.wait_ge(*ro_a.at(f"x{tb - 2}", b))
                    elif before:
                        pe.wait_ge(*n1_a.at(f"raw{tb + 2}", b + 2))
                    else:
                        pe.wait_ge(*ro_a.at(f"h{tb}", b - 1))
                        pe.wait_ge(*qt_a.at(f"q{tb + 2}", bl))
                    for c in range(C):
                        m = pe.transpose(w[:, c * P:(c + 1) * P], x2[b.slot][:, tb, c * P:(c + 1) * P], ident)
                    m.then_inc(ro_t(f"x{tb}"), 1)

            def router_stats(b, before):
                pe.wait_ge(*ro_v.at("stats", b))
                if before:
                    pe.wait_ge(*ga_a.at("fx", b + 2))
                else:
                    pe.wait_ge(*ga_a.at("gcol", bl))
                    pe.wait_ge(*ro_a.at("lg", b - 1))
                for tb in range(TB):
                    m = pe.transpose(Tb[0:NSTAT, tb * P:(tb + 1) * P], st6[:, tb, :], ident)
                m.then_inc(ro_t("st"), 1)

            def router_hidden(b, k, before):
                pe.wait_ge(*ro_a.at(f"x{TB - 1}", b))
                if before:
                    pe.wait_ge(*qt_a.at(f"q{k + 2}", b + 2))
                for c in range(C):
                    pe.matmul(Wb[k][:, :], r1x[:, c, k * P:(k + 1) * P], x2T[:, c, :], start=(c == 0), stop=False)

            def router_hidden_stats(b):
                pe.wait_ge(*ro_a.at("st", b))
                for k in range(RM):
                    pe.matmul(Wb[k][:, :], r1s[:, k * P:(k + 1) * P], stT, start=False, stop=True)\
                        .then_inc(ro_t(f"h{k}"), 1)

            def router_logits(b):
                pe.wait_ge(*ro_a.at("h1", b))
                for tb in range(TB):
                    for k in range(RM):
                        m = pe.matmul(Tb[:, tb * NE:(tb + 1) * NE], hg[:, k, tb * P:(tb + 1) * P], r2[:, k, :],
                                      start=(k == 0), stop=(k == RM - 1))
                m.then_inc(ro_t("lg"), 1)

            def step(n, a, s, r, x1, x2):
                for h in range(NH):
                    if s:
                        if h + 2 < NH:
                            broadcast_max(n - 1, h + 2)
                        if h:
                            scores(n - 1, h, (2,))
                        if h + 1 < NH:
                            scores(n - 1, h + 1, (0,))
                    if a:
                        if h == 0:
                            retention(n, 0)
                            retention(n, 1)
                        if h == 1:
                            gates_k(n)
                        if h == 2:
                            retention(n, 2)
                            retention(n, 3)
                        if h == 4:
                            queries(n)
                            gates_q(n)
                    if r:
                        if h == 3:
                            router_in(n - 2, a)
                        if h in (5, 6):
                            router_hidden(n - 2, h - 5, a)
                        if h == 5:
                            router_stats(n - 2, a)
                        if h == 6:
                            router_hidden_stats(n - 2)
                        if h == 7:
                            router_logits(n - 2)
                    if a and h == 7:
                        gate_columns(n)
                        broadcast_max(n, 0)
                    if s:
                        if h + 1 < NH:
                            scores(n - 1, h + 1, (1,))
                        values(n - 1, h)
                if a:
                    scores(n, 0, (0, 1))
                    broadcast_max(n, 1)
                    scores(n, 0, (2,))

            run_pipeline(pe, step)

            pe.wait_ge(*ro_v.at("save", bl))
            for half in range(2):
                for k in range(4):
                    m = pe.transpose(Wb[half][:, k * P:(k + 1) * P], sc_all[:, half * 4 + k, :], ident)
                m.then_inc(se_t(f"scT{half}"), 1)
            pe.wait_ge(*se_p.at("iotas", b0))
            for i in range(NSEL):
                pe.wait_ge(*se_v.at(f"cmp{i}", b0))
                pe.matmul(Tb[:, 0:1], blk, cnt, start=True, stop=True).then_inc(se_t(f"cnt{i}"), 1)
            last = slice(P - 1, P)
            for name, w, after, col in (("gtc", blk, "gt", cnt), ("eqo", low, "eqscan", cmpb[:, NT // 4 - 1, last]),
                                        ("selo", low, "scan", pos[:, NT // 4 - 1, last])):
                pe.wait_ge(*se_v.at(after, b0))
                pe.matmul(Tb[:, 0:1], w, col, start=True, stop=True).then_inc(se_t(name), 1)
            pe.wait_ge(*se_v.at("masked", b0))
            for half in range(2):
                for k in range(4):
                    m = pe.transpose(Wb[half][:, k * P:(k + 1) * P], pos[:, half * 4 + k, :], ident)
                m.then_inc(se_t(f"posT{half}"), 1)
            for i in range(2 * NT // LG):
                pe.wait_ge(*li_v.at(f"t{i}", b0))
                for j in range(LG):
                    m = pe.matmul(Tb[:, 0:4 * NE], Lh[i % 2][:, j], Hh[i % 2][:, j].rearrange("p a b -> p (a b)"),
                                  start=(i + j == 0), stop=(i * LG + j == 2 * NT - 1))
                m.then_inc(li_t(f"m{i}"), 1)

            def rows_in(e):
                pe.wait_ge(ld_g[e.slot], e.landed(2))
                for k in range(2):
                    pe.wait_ge(*xr_a.at(f"x{k}", e - 1))
                    for c in range(2):
                        ch = slice((2 * k + c) * P, (2 * k + c + 1) * P)
                        pe.transpose(Xb[k][:, c * CAP:c * CAP + P], xg[e.slot][:, 0, ch], ident)
                        m = pe.transpose(Xb[k][:, c * CAP + P:(c + 1) * CAP], xg[e.slot][0:CAP2, 1, ch],
                                         ident[0:CAP2, 0:CAP2])
                    m.then_inc(xr_t(f"x{k}"), 1)

            def up(e, j):
                if j == 0:
                    pe.wait_ge(ld_wu[e.slot], e.landed())
                    pe.wait_ge(*xr_a.at("x1", e))
                if j == J:
                    pe.wait_ge(ld_au[e.slot], e.landed())
                if j < 2:
                    pe.wait_ge(*up_v.at(f"mul{J - 1 + j}", e - 1))
                else:
                    pe.wait_ge(*up_v.at(f"mul{j - 2}", e))
                u = Ub[(e.slot * (J + 1) + j) % 2]
                for g in range(2):
                    for c in range(C):
                        w = wu[e.slot][:, c, g * INTER + j * P:g * INTER + (j + 1) * P] if j < J else \
                            au[e.slot][:, c, g * AINT:(g + 1) * AINT]
                        m = pe.matmul(u[:, g * CAP:(g + 1) * CAP], w, xeT[:, c, :], start=(c == 0), stop=(c == C - 1))
                m.then_inc(up_t(f"up{j}"), 1)

            def down(e):
                pe.wait_ge(ld_wd[e.slot], e.landed())
                pe.wait_ge(ld_ad[e.slot], e.landed())
                pe.wait_ge(*up_v.at(f"mul{J}", e))
                for k in range(2):
                    pe.wait_ge(*dn_a.at(f"d{k}", e - 1))
                    for c in range(2):
                        ch = slice((2 * k + c) * P, (2 * k + c + 1) * P)
                        for j in range(J + 1):
                            w = wd[e.slot][:, j, ch] if j < J else ad[e.slot][:, ch]
                            m = pe.matmul(Db[k][:, c * CAP:(c + 1) * CAP], w, hact[:, j, :], start=(j == 0), stop=(j == J))
                    m.then_inc(dn_t(f"d{k}"), 1)

            def rows_out(e):
                pe.wait_ge(*dn_a.at("d1", e))
                for k in range(2):
                    pe.wait_ge(*yr_v.at(f"y{k}", e - 1))
                    for c in range(C):
                        if k == 0:
                            m = pe.transpose(Yb[0][:, c * P:(c + 1) * P], yT[:, c, 0:P], ident)
                        else:
                            m = pe.transpose(Yb[1][0:CAP2, c * P:(c + 1) * P], yT[:, c, P:CAP], ident)
                    m.then_inc(yr_t(f"y{k}"), 1)

            def expert(e, first, last_):
                up(e, 0)
                if not first:
                    rows_out(e - 1)
                for j in range(1, J + 1):
                    up(e, j)
                if not last_:
                    rows_in(e + 1)
                down(e)

            rows_in(b0)
            run_experts(pe, expert)
            rows_out(Batch(0, NE - 1))

        @block.scalar
        def _(act):
            start(act, "scalar")
            act.wait_ge(ld_first, 64)
            act.activation(a_dec, a_dec, ACT.Exp, scale=-1.0).then_inc(cs_a("dec"), 1)
            act.wait_ge(*cs_v.at("tap", b0))

            def inputs(b, c):
                if c == 0:
                    act.wait_ge(ld_x, b.line(16, 16))
                    act.wait_ge(*re_t.at(f"w{TB - 1}", b - 1))
                act.activation(ST[:, c, :], xc[:, c, :], ACT.Identity, scale=a_one[:, c:c + 1])\
                    .then_inc(re_a(f"u{c}"), 1)
                act.activation(cv[:, c, :], xc[:, c, :], ACT.Identity, scale=cw[:, c, PAD:PAD + 1],
                               bias=cb[:, c:c + 1]).then_inc(re_a(f"cv{c}"), 1)

            def raw_rows(b, tb):
                if tb == 0:
                    act.wait_ge(*l2_v.at("sum", b - 2))
                    act.wait_ge(*qt_t.at(f"t{TB - 1}", b - 2))
                act.wait_ge(*re_t.at(f"w{tb}", b))
                act.activation(x1[b.slot][:, tb, :], Wb[tb % 2][:, :], ACT.Copy).then_inc(n1_a(f"raw{tb}"), 1)

            def queries(b):
                act.wait_ge(*at_t.at(f"s{NH - 1}_2", b - 2))
                for tb in range(TB):
                    act.wait_ge(*qt_t.at(f"t{tb}", b))
                    act.activation(qT[b.slot][:, :, tb * P:(tb + 1) * P],
                                   Wb[tb % 2][:, :].rearrange("p (c t) -> p c t", c=C), ACT.Copy)\
                        .then_inc(qt_a(f"q{tb}"), 1)

            def gates_1(b):
                act.wait_ge(*ga_v.at("lo", b - 1))
                act.wait_ge(*ga_t.at("gates", b))
                act.activation(g_ig[0:NH], Tb[0:NH, :], ACT.Identity, bias=gbias[0:NH]).then_inc(ga_a("ig"), 1)
                act.activation(g_fx[0:NH], Tb[32:GATE, :], ACT.Identity, bias=gbias[32:GATE]).then_inc(ga_a("fx"), 1)

            def gates_2(b):
                act.wait_ge(*ga_v.at("abs", b))
                act.activation(g_ab[0:NH], g_ab[0:NH], ACT.Exp, scale=-1.0).then_inc(ga_a("exp"), 1)
                act.wait_ge(*ga_a.at("exp", b))
                act.activation(g_l[0:NH], g_ab[0:NH], ACT.Ln, bias=1.0).then_inc(ga_a("log"), 1)

            def gates_3(b):
                act.wait_ge(*ga_v.at("max", b))
                act.wait_ge(*bc_t.at(f"bc{NH - 1}", b - 2))
                act.activation(bfs[b.slot][0:NH], g_m[0:NH], ACT.Copy, scale=-1.0).then_inc(ga_a("hi"), 1)

            def gates_4(b):
                act.wait_ge(*ga_v.at("r1", b))
                act.activation(g_m0[0:NH], g_r[0:NH], ACT.Copy).then_inc(ga_a("m0"), 1)
                act.activation(bfs[b.slot][32:GATE], g_r[0:NH], ACT.Copy).then_inc(ga_a("mid"), 1)

            def gates_5(b):
                act.wait_ge(*ga_t.at("cols", b))
                act.wait_ge(*ev_v.at(f"den{NH - 1}", b - 2))
                act.wait_ge(*at_a.at(f"exp{NH - 1}", b - 2))
                act.activation(gcol[b.slot], Tb[:, 0:TB * GATE].rearrange("p (a g) -> p a g", a=TB), ACT.Copy)\
                    .then_inc(ga_a("gcol"), 1)
                act.wait_ge(*ga_a.at("gcol", b))
                act.activation(ng[b.slot], gcol[b.slot][:, :, 0:NH], ACT.Copy, scale=-1.0).then_inc(ga_a("ng"), 1)
                act.activation(en[b.slot], gcol[b.slot][:, :, 32:GATE], ACT.Exp).then_inc(ga_a("en"), 1)

            def decays(b, h):
                act.wait_ge(*bc_t.at(f"bc{h}", b))
                if h >= ND:
                    act.wait_ge(*pv_t.at(f"pv{h - ND}", b))
                else:
                    former = max(k for k in range(NH) if k % ND == h)
                    act.wait_ge(*pv_t.at(f"pv{former}", b - 1))
                if h == 0:
                    act.wait_ge(*ga_a.at("en", b))
                for tb in range(TB):
                    m = act.activation(Dm[h % ND][:, tb * P:(tb + 1) * P], Bb[:, tb * P:(tb + 1) * P], ACT.Relu,
                                       scale=-1.0, bias=ng[b.slot][:, tb, h:h + 1])
                m.then_inc(at_a(f"relu{h}"), 1)
                for tb in range(TB - 1):
                    act.activation(Dm[h % ND][:, AFTER[tb]:AFTER[tb] + AFTERW[tb]], Bb[:, (tb + 1) * P:], ACT.Exp,
                                   bias=gcol[b.slot][:, tb, h:h + 1])
                act.wait_ge(*at_a.at(f"relu{h}", b))
                act.activation(Dm[h % ND][:, 0:TB * P], Dm[h % ND][:, 0:TB * P], ACT.Exp, scale=-1.0)\
                    .then_inc(at_a(f"exp{h}"), 1)

            def router_1(b):
                act.wait_ge(*ro_t.at("h1", b - 1))
                for tb in range(TB):
                    act.wait_ge(*ro_t.at(f"x{tb}", b))
                    act.activation(x2T[:, :, tb * P:(tb + 1) * P],
                                   Wb[tb % 2][:, :].rearrange("p (c t) -> p c t", c=C), ACT.Copy)\
                        .then_inc(ro_a(f"x{tb}"), 1)

            def router_stats(b):
                act.wait_ge(*ro_t.at("st", b))
                act.activation(stT[0:NSTAT], Tb[0:NSTAT, :], ACT.Copy).then_inc(ro_a("st"), 1)

            def router_2(b, k):
                act.wait_ge(*ro_t.at("lg", b - 1))
                act.wait_ge(*ro_t.at(f"h{k}", b))
                act.activation(hg[:, k, :], Wb[k][:, :], ACT.Gelu, bias=r1b[:, k:k + 1]).then_inc(ro_a(f"h{k}"), 1)

            def router_3(b):
                act.wait_ge(*ro_t.at("lg", b))
                act.wait_ge(*ro_v.at("lsub", b - 1))
                act.activation(lg, Tb[:, 0:TB * NE].rearrange("p (a e) -> p a e", a=TB), ACT.Copy)\
                    .then_inc(ro_a("lg"), 1)

            def router_4(b):
                act.wait_ge(*ro_v.at("lsub", b))
                act.activation(pr, pr, ACT.Exp).then_inc(ro_a("exp"), 1)

            def step(n, a, s, r, x1, x2):
                for h in range(NH):
                    if s and h + 2 < NH:
                        decays(n - 1, h + 2)
                    if a and h in (1, 2):
                        raw_rows(n, 2 * h - 2)
                        raw_rows(n, 2 * h - 1)
                    if r and h == 3:
                        router_1(n - 2)
                    if h == 3 and x1 and not s:
                        for c in range(C):
                            inputs(n + 1, c)
                    if a and h == 4:
                        queries(n)
                        gates_1(n)
                    if r and h == 5:
                        router_stats(n - 2)
                    if a:
                        if h == 5:
                            gates_2(n)
                        if h == 6:
                            gates_3(n)
                            gates_4(n)
                    if r and h == 6:
                        router_2(n - 2, 0)
                        router_2(n - 2, 1)
                    if NH - C - 1 <= h < NH - 1 and x1 and s:
                        inputs(n + 1, h - (NH - C - 1))
                    if r and h == 7:
                        router_3(n - 2)
                if a:
                    gates_5(n)
                    decays(n, 0)
                if r:
                    router_4(n - 2)
                if a:
                    decays(n, 1)

            for c in range(C):
                inputs(b0, c)
            act.wait_ge(ld_c, 16 * NCONST)
            run_pipeline(act, step)

            def rows_in(e):
                act.wait_ge(*up_t.at(f"up{J}", e - 1))
                for k in range(2):
                    act.wait_ge(*xr_t.at(f"x{k}", e))
                    act.activation(xeT[:, 2 * k:2 * k + 2, :],
                                   Xb[k][:, 0:2 * CAP].rearrange("p (c t) -> p c t", c=2), ACT.Copy)\
                        .then_inc(xr_a(f"x{k}"), 1)

            def expert(e, first, last):
                for j in range(J + 1):
                    act.wait_ge(*up_t.at(f"up{j}", e))
                    if j >= 2:
                        act.wait_ge(*up_v.at(f"mul{j - 2}", e))
                    else:
                        act.wait_ge(*up_v.at(f"mul{J - 1 + j}", e - 1))
                    k = (e.slot * (J + 1) + j) % 2
                    act.activation(sg[k], Ub[k][:, 0:CAP], ACT.Silu).then_inc(up_a(f"silu{j}"), 1)
                if not last:
                    rows_in(e + 1)
                act.wait_ge(*yr_t.at("y1", e - 1))
                for k in range(2):
                    act.wait_ge(*dn_t.at(f"d{k}", e))
                    act.activation(yT[:, 2 * k:2 * k + 2, :],
                                   Db[k][:, 0:2 * CAP].rearrange("p (c t) -> p c t", c=2), ACT.Copy)\
                        .then_inc(dn_a(f"d{k}"), 1)

            rows_in(b0)
            run_experts(act, expert)

        @block.vector
        def _(dve):
            start(dve, "vector")
            for t in (xT[:, :, 0:PAD], xT[:, :, PAD + T:], wgq, wgk, wgv, gm, stT, r1s, bfs[0], bfs[1], zeros):
                dve.memset(t, 0.0)
            for t in va:
                dve.memset(t[:, :, NH * VW:], 0.0)
                dve.memset(t[:, :, 0:NH * VW].rearrange("p a (h w) -> p a h w", h=NH)[:, :, :, DH:VW], 1.0)
            dve.memset(negh, -0.5)
            dve.memset(posh, 0.5)
            dve.memset(ones, 1.0).then_inc(cs_v("misc"), 1)
            dve.wait_ge(ld_first, 64)
            dve.wait_ge(*cs_a.at("dec", b0))
            dve.tensor_scalar(a_dec, a_dec, 1.0, None, ALU.add).then_inc(cs_v("dec1"), 1)
            dve.wait_ge(*cs_v.at("dec1", b0))
            dve.reciprocal(a_dec, a_dec).then_inc(cs_v("dec2"), 1)
            dve.wait_ge(*cs_v.at("dec2", b0))
            dve.tensor_scalar(a_one, a_dec, -1.0, 1.0, ALU.mult, ALU.add)
            dve.tensor_tensor(cb, cb, rb, ALU.add)
            dve.tensor_scalar(cw[:, :, PAD:PAD + 1], cw[:, :, PAD:PAD + 1], 1.0, None, ALU.add).then_inc(cs_v("tap"), 1)
            dve.wait_ge(*cs_v.at("tap", b0))

            def retained(b, c):
                dve.wait_ge(*re_a.at(f"u{c}", b))
                dve.tensor_tensor_scan(ST[:, c, :], a_dec[:, c:c + 1].to_broadcast([P, T]), ST[:, c, :], 0.0,
                                       ALU.mult, ALU.add).then_inc(re_v(f"scan{c}"), 1)
                dve.wait_ge(*re_a.at(f"cv{c}", b))
                for i, k in enumerate(k for k in range(TAPS) if k != PAD):
                    if i:
                        dve.wait_ge(*re_v.at(f"tap{i - 1}_{c}", b))
                    dve.scalar_tensor_tensor(cv[:, c, :], xT[:, c, k:k + T], cw[:, c, k:k + 1], cv[:, c, :],
                                             ALU.mult, ALU.add).then_inc(re_v(f"tap{i}_{c}"), 1)

            def norm1_stats(b, tb):
                if tb == 0:
                    dve.wait_ge(*n1_v.at(f"out{TB - 1}", b - 1))
                dve.wait_ge(*n1_a.at(f"raw{tb}", b))
                dve.bn_stats(bn1[:, tb, :], x1[b.slot][:, tb, :]).then_inc(n1_v(f"bn{tb}"), 1)

            def norm1(b):
                dve.wait_ge(*n1_v.at(f"bn{TB - 1}", b))
                hold(dve)
                for tb in range(TB):
                    m = dve.bn_aggr(mv1[:, tb, :], bn1[:, tb, :])
                m.then_inc(n1_v("aggr"), 1)

            def norm1_out(b):
                dve.wait_ge(*n1_p.at("rstd", b))
                for tb in range(TB):
                    dve.tensor_scalar(x1[b.slot][:, tb, :], x1[b.slot][:, tb, :], mv1[:, tb, 0:1], rs1[:, tb:tb + 1],
                                      ALU.subtract, ALU.mult).then_inc(n1_v(f"out{tb}"), 1)

            def weigh(b, h, chunks):
                dve.wait_ge(*at_p.at(f"mask{h}", b))
                for i in chunks:
                    at, n = ((0, 512), (512, 384), (896, 384))[i]
                    dve.wait_ge(*at_t.at(f"s{h}_{i}", b))
                    d = Dm[h % ND][:, at:at + n]
                    dve.scalar_tensor_tensor(d, Sb[(3 * h + i) % 2][:, 0:n], DH ** -0.5, d, ALU.mult, ALU.mult)\
                        .then_inc(at_v(f"mul{h}_{i}"), 1)

            def head_out(b, h):
                pv = Pb[h % 2][:, 0:TB * PVN].rearrange("p (a w) -> p a w", a=TB)
                dve.wait_ge(*pv_t.at(f"pv{h}", b))
                if h == 0:
                    dve.wait_ge(*ga_a.at("en", b))
                    dve.wait_ge(*ro_t.at(f"x{TB - 1}", b - 2))
                    dve.wait_ge(*ro_v.at("stats", b - 2))
                    dve.wait_ge(st_x2[b.slot], b.landed())
                    dve.wait_ge(st_acc[b.slot], b.landed())
                if h:
                    dve.wait_ge(*ev_v.at(f"out{h - 1}", b))
                else:
                    dve.wait_ge(*ev_v.at(f"out{NH - 1}", b - 1))
                dve.scalar_tensor_tensor(den, pv[:, :, DH], -1.0, en[b.slot][:, :, h], ALU.mult, ALU.max)\
                    .then_inc(ev_v(f"neg{h}"), 1)
                dve.wait_ge(*ev_v.at(f"neg{h}", b))
                dve.tensor_tensor(den, pv[:, :, DH], den, ALU.max).then_inc(ev_v(f"den{h}"), 1)
                dve.wait_ge(*ev_v.at(f"den{h}", b))
                dve.tensor_scalar(den, den, CELL_EPS, None, ALU.add).then_inc(ev_v(f"eps{h}"), 1)
                dve.wait_ge(*ev_v.at(f"eps{h}", b))
                dve.reciprocal(den, den).then_inc(ev_v(f"rec{h}"), 1)
                dve.wait_ge(*ev_v.at(f"rec{h}", b))
                dve.tensor_tensor(x2[b.slot][:, :, h * DH:(h + 1) * DH], pv[:, :, 0:DH],
                                  den.unsqueeze(2).to_broadcast([P, TB, DH]), ALU.mult).then_inc(ev_v(f"out{h}"), 1)

            def norm2_stats(b):
                dve.wait_ge(*l2_v.at(f"out{TB - 1}", b - 1))
                dve.wait_ge(*ev_v.at(f"out{NH - 1}", b))
                for tb in range(TB):
                    m = dve.bn_stats(bn2[:, tb, :], x2[b.slot][:, tb, :])
                m.then_inc(l2_v("bn2"), 1)
                dve.wait_ge(*l2_v.at("bn2", b))
                hold(dve)
                for tb in range(TB):
                    m = dve.bn_aggr(mv2[:, tb, :], bn2[:, tb, :])
                m.then_inc(l2_v("aggr2"), 1)
                dve.wait_ge(*l2_v.at("aggr2", b))
                for tb in range(TB):
                    m = dve.scalar_tensor_tensor(x2[b.slot][:, tb, :], x2[b.slot][:, tb, :], mv2[:, tb, 0:1], lns, ALU.subtract, ALU.mult)
                m.then_inc(l2_v("scaled"), 1)

            def norm3_stats(b):
                dve.wait_ge(*l2_v.at("scaled", b))
                dve.wait_ge(*l2_p.at("rstd2", b))
                for tb in range(TB):
                    m = dve.scalar_tensor_tensor(x2[b.slot][:, tb, :], x2[b.slot][:, tb, :], rs2[:, tb:tb + 1], x1[b.slot][:, tb, :],
                                                 ALU.mult, ALU.add)
                m.then_inc(l2_v("sum"), 1)
                dve.wait_ge(*l2_v.at("sum", b))
                for tb in range(TB):
                    m = dve.bn_stats(bn3[:, tb, :], x2[b.slot][:, tb, :])
                m.then_inc(l2_v("bn3"), 1)
                dve.wait_ge(*l2_v.at("bn3", b))
                hold(dve)
                for tb in range(TB):
                    m = dve.bn_aggr(mv3[:, tb, :], bn3[:, tb, :])
                m.then_inc(l2_v("aggr3"), 1)

            def norm3_out(b):
                dve.wait_ge(*l2_p.at("rstd3", b))
                for tb in range(TB):
                    dve.tensor_scalar(x2[b.slot][:, tb, :], x2[b.slot][:, tb, :], mv3[:, tb, 0:1], rs3[:, tb:tb + 1],
                                      ALU.subtract, ALU.mult).then_inc(l2_v(f"out{tb}"), 1)

            def gates_1(b):
                dve.wait_ge(*ga_a.at("fx", b))
                dve.scalar_tensor_tensor(g_ab[0:NH], g_fx[0:NH], -1.0, g_fx[0:NH], ALU.mult, ALU.max).then_inc(ga_v("abs"), 1)
                dve.tensor_scalar(g_mn[0:NH], g_fx[0:NH], 0.0, None, ALU.min).then_inc(ga_v("min"), 1)

            def gates_2(b):
                dve.wait_ge(*ga_a.at("log", b))
                dve.wait_ge(*ga_v.at("min", b))
                dve.tensor_tensor(g_lf[0:NH], g_mn[0:NH], g_l[0:NH], ALU.subtract).then_inc(ga_v("logf"), 1)
                dve.wait_ge(*ga_v.at("logf", b))
                dve.tensor_tensor_scan(g_cs[0:NH], ones[0:NH].to_broadcast([NH, T]), g_lf[0:NH], 0.0,
                                       ALU.mult, ALU.add).then_inc(ga_v("cum"), 1)
                dve.wait_ge(*ga_v.at("cum", b))
                dve.wait_ge(*ga_t.at("cols", b - 1))
                dve.tensor_tensor(gm[0:NH], g_ig[0:NH], g_cs[0:NH], ALU.subtract).then_inc(ga_v("g"), 1)
                dve.wait_ge(*ga_v.at("g", b))
                dve.tensor_tensor_scan(g_m[0:NH], gm[0:NH], gm[0:NH], -3.0e38, ALU.max, ALU.max).then_inc(ga_v("max"), 1)
                dve.wait_ge(*ga_v.at("max", b))
                dve.scalar_tensor_tensor(gm[32:GATE], g_cs[0:NH], -1.0, g_m[0:NH], ALU.mult, ALU.subtract)\
                    .then_inc(ga_v("neg"), 1)

            def gates_3(b):
                dve.wait_ge(*ga_a.at("hi", b))
                dve.scalar_tensor_tensor(g_r[0:NH], g_m[0:NH], -1.0, bfs[b.slot][0:NH], ALU.mult, ALU.subtract)\
                    .then_inc(ga_v("r1"), 1)

            def gates_4(b):
                dve.wait_ge(*ga_a.at("m0", b))
                dve.tensor_tensor(bfs[b.slot][64:64 + NH], g_r[0:NH], g_m0[0:NH], ALU.subtract).then_inc(ga_v("lo"), 1)

            def router_stats(b, part):
                if part == 0:
                    dve.wait_ge(*l2_v.at(f"out{TB - 1}", b))
                    dve.wait_ge(*ro_t.at("st", b - 1))
                    for tb in range(TB):
                        m = dve.bn_stats(bnr[:, tb, :], x2[b.slot][:, tb, :])
                    m.then_inc(ro_v("bn"), 1)
                    dve.wait_ge(*ro_v.at("bn", b))
                    hold(dve)
                    for tb in range(TB):
                        m = dve.bn_aggr(mvr[:, tb, :], bnr[:, tb, :])
                    m.then_inc(ro_v("aggr"), 1)
                if part == 1:
                    dve.wait_ge(*ro_v.at("aggr", b))
                    dve.tensor_tensor(vr[:, 1, :], mvr[:, :, 0], mvr[:, :, 0], ALU.mult).then_inc(ro_v("sq"), 1)
                    dve.wait_ge(*ro_v.at("sq", b))
                    dve.tensor_tensor(vr[:, 1, :], vr[:, 1, :], mvr[:, :, 1], ALU.add).then_inc(ro_v("sum"), 1)
                    dve.wait_ge(*ro_v.at("sum", b))
                    dve.tensor_scalar(vr[:, 1, :], vr[:, 1, :], float(D), None, ALU.mult)
                    dve.tensor_scalar(vr[:, 0, :], mvr[:, :, 1], D / (D - 1.0), None, ALU.mult).then_inc(ro_v("vars"), 1)
                if part == 2:
                    dve.tensor_reduce(st6[:, :, 2], x2[b.slot], AX.X, ALU.min)
                if part == 3:
                    dve.tensor_reduce(st6[:, :, 3], x2[b.slot], AX.X, ALU.max)
                if part == 4:
                    dve.wait_ge(st_dum, 64)
                    for tb in range(TB):
                        m = dve.tensor_scalar(junk[:, tb, :], x2[b.slot][:, tb, :], -SPARSE, None, ALU.is_gt)
                    m.then_inc(ro_v("above"), 1)
                    dve.wait_ge(*ro_v.at("above", b))
                    for tb in range(TB):
                        m = dve.scalar_tensor_tensor(junk[:, tb, :], x2[b.slot][:, tb, :], SPARSE, junk[:, tb, :], ALU.is_lt,
                                                     ALU.mult, accum_out=nz[:, tb:tb + 1])
                    m.then_inc(ro_v("cnt"), 1)
                    dve.wait_ge(*ro_v.at("cnt", b))
                    dve.tensor_scalar(st6[:, :, 5], nz, 1.0 / D, None, ALU.mult)
                    dve.tensor_copy(st6[:, :, 0], mvr[:, :, 0])
                    dve.wait_ge(*ro_p.at("l2", b))
                    dve.tensor_copy(st6[:, :, 1], vr[:, 0, :])
                    dve.tensor_copy(st6[:, :, 4], vr[:, 1, :]).then_inc(ro_v("stats"), 1)

            def softmax_1(b):
                dve.wait_ge(*ro_a.at("lg", b))
                dve.wait_ge(*ro_v.at("save", b - 1))
                dve.tensor_reduce(nmx, lg, AX.X, ALU.max).then_inc(ro_v("lmax"), 1)
                dve.wait_ge(*ro_v.at("lmax", b))
                dve.tensor_tensor(pr, lg, nmx.unsqueeze(2).to_broadcast([P, TB, NE]), ALU.subtract)\
                    .then_inc(ro_v("lsub"), 1)

            def softmax_2(b):
                dve.wait_ge(*ro_a.at("exp", b))
                dve.tensor_reduce(wsum, pr, AX.X, ALU.add).then_inc(ro_v("lsum"), 1)
                dve.wait_ge(*ro_v.at("lsum", b))
                dve.reciprocal(wsum, wsum).then_inc(ro_v("lrec"), 1)
                dve.wait_ge(*ro_v.at("lrec", b))
                dve.tensor_tensor(pr, pr, wsum.unsqueeze(2).to_broadcast([P, TB, NE]), ALU.mult)\
                    .then_inc(ro_v("prob"), 1)
                dve.wait_ge(*ro_v.at("prob", b))

            def top_two(b):
                hold(dve)
                for tb in range(TB):
                    m = dve.max(top8[:, tb, :], pr[:, tb, :])
                m.then_inc(ro_v("top"), 1)
                dve.wait_ge(*ro_v.at("top", b))
                hold(dve)
                for tb in range(TB):
                    m = dve.max_index(at8[:, tb, :], top8[:, tb, :], pr[:, tb, :])
                m.then_inc(ro_v("at"), 1)
                dve.tensor_tensor(wsum, top8[:, :, 0], top8[:, :, 1], ALU.add).then_inc(ro_v("sum2"), 1)
                dve.wait_ge(*ro_v.at("sum2", b))
                dve.tensor_copy(ex2, at8[:, :, 0:2])
                dve.reciprocal(wsum, wsum).then_inc(ro_v("rec2"), 1)
                dve.wait_ge(*ro_v.at("rec2", b))
                io = iota_e.unsqueeze(1).to_broadcast([P, TB, NE])
                dve.tensor_tensor(oh0, io, ex2[:, :, 0:1].to_broadcast([P, TB, NE]), ALU.is_equal)
                dve.tensor_tensor(oh1, io, ex2[:, :, 1:2].to_broadcast([P, TB, NE]), ALU.is_equal)
                dve.tensor_copy(tiles_of(e_all, b), ex2)
                dve.tensor_tensor(tiles_of(w_all, b), top8[:, :, 0:2], wsum.unsqueeze(2).to_broadcast([P, TB, 2]),
                                  ALU.mult).then_inc(ro_v("oh"), 1)
                dve.wait_ge(*ro_v.at("oh", b))
                dve.tensor_tensor(oh0, oh0, oh1, ALU.add).then_inc(ro_v("ohs"), 1)
                dve.wait_ge(*ro_v.at("ohs", b))
                pair = (b - b.slot).line(NE // 2)
                dve.tensor_tensor(sc_all[:, b.slot * TB:(b.slot + 1) * TB, bass.ds(pair, NE)], oh0, pr, ALU.mult)\
                    .then_inc(ro_v("save"), 1)

            def tiles_of(ap, b):
                return ap.rearrange("p (n a) e -> p n a e", a=TB)[:, b.line(1)]

            def step(n, a, s, r, x1, x2):
                for h in range(NH):
                    if s and h:
                        weigh(n - 1, h, (0, 1))
                    if r:
                        if h == 0:
                            norm2_stats(n - 2)
                        if h == 1:
                            norm3_stats(n - 2)
                        if h == 2:
                            norm3_out(n - 2)
                            router_stats(n - 2, 0)
                        if h == 3:
                            router_stats(n - 2, 2)
                        if h == 4:
                            router_stats(n - 2, 3)
                    if a and h == 7:
                        gates_4(n)
                    if h in (5, 6) and x1 and s:
                        retained(n + 1, 2 * (h - 5))
                    if s and h:
                        weigh(n - 1, h, (2,))
                        head_out(n - 1, h - 1)
                    if a and h in (2, 3):
                        norm1_stats(n, 2 * h - 4)
                        norm1_stats(n, 2 * h - 3)
                    if a and h == 3:
                        norm1(n)
                    if r and h == 3:
                        router_stats(n - 2, 1)
                    if a and h == 3:
                        norm1_out(n)
                    if h == 4 and x1 and not s:
                        for c in range(C):
                            retained(n + 1, c)
                    if r and h == 4:
                        router_stats(n - 2, 4)
                    if a:
                        if h == 5:
                            gates_1(n)
                        if h == 6:
                            gates_2(n)
                            gates_3(n)
                    if h in (5, 7) and x1 and s:
                        retained(n + 1, h - 4)
                if s:
                    head_out(n - 1, NH - 1)
                if r:
                    softmax_1(n - 2)
                if a:
                    weigh(n, 0, (0, 1))
                if r:
                    softmax_2(n - 2)
                    top_two(n - 2)
                if a:
                    weigh(n, 0, (2,))

            for c in range(C):
                retained(b0, c)
                if c == 0:
                    dve.wait_ge(ld_c, 16 * NCONST)
                    dve.tensor_tensor(wgk, wgk, wgv, ALU.add).then_inc(cs_v("gkv"), 1)
            run_pipeline(dve, step)

            dve.wait_ge(*ro_v.at("save", bl))
            dve.wait_ge(*se_p.at("iotas", b0))
            for half in range(2):
                dve.wait_ge(*se_t.at(f"scT{half}", b0))
                dve.tensor_copy(scT[:, half * 4:half * 4 + 4, :], Wb[half][:, :].rearrange("p (k t) -> p k t", k=4))\
                    .then_inc(se_v(f"scT{half}"), 1)
            dve.memset(thr, 1 << MAXBIT).then_inc(se_v("thr"), 1)
            dve.wait_ge(*se_v.at("scT1", b0))
            upper = scT.rearrange("p a b -> p (a b)").bitcast(BF16).rearrange("p (n k) -> p n k", k=2)[:, :, 1]
            dve.tensor_copy(scH, upper).then_inc(se_v("upper"), 1)
            dve.wait_ge(*se_v.at("upper", b0))
            thf = thr.bitcast(F32)
            for i in range(NSEL):
                src, out = (scH, cmpH) if MAXBIT - i >= 16 else (scT, cmpb)
                dve.tensor_scalar(out, src, thf, None, ALU.is_ge, ALU.add, accum_out=cnt).then_inc(se_v(f"cmp{i}"), 1)
                dve.wait_ge(*se_t.at(f"cnt{i}", b0))
                dve.tensor_scalar(bit, Tb[:, 0:1], float(CAP), float(1 << (MAXBIT - i)), ALU.is_lt, ALU.mult)\
                    .then_inc(se_v(f"bit{i}"), 1)
                dve.wait_ge(*se_v.at(f"bit{i}", b0))
                below = 1 << (MAXBIT - i - 1) if i < NSEL - 1 else 0
                dve.scalar_tensor_tensor(thr, bit, below, thr, ALU.bitwise_xor, ALU.bitwise_xor)\
                    .then_inc(se_v(f"thr{i}"), 1)
                dve.wait_ge(*se_v.at(f"thr{i}", b0))
            dve.tensor_scalar(gt, scT, thf, None, ALU.is_gt, ALU.add, accum_out=cnt).then_inc(se_v("gt"), 1)
            dve.wait_ge(*se_t.at("gtc", b0))
            dve.tensor_scalar(need, Tb[:, 0:1], -1.0, float(CAP), ALU.mult, ALU.add).then_inc(se_v("need"), 1)
            dve.tensor_scalar(off, thf, 0.0, 2.0, ALU.is_equal, ALU.mult).then_inc(se_v("off"), 1)
            dve.wait_ge(*se_v.at("off", b0))
            dve.tensor_tensor(off, off, thf, ALU.add).then_inc(se_v("eqthr"), 1)
            dve.wait_ge(*se_v.at("eqthr", b0))
            dve.tensor_scalar(eq, scT, off, None, ALU.is_equal).then_inc(se_v("eq"), 1)
            dve.wait_ge(*se_v.at("eq", b0))

            def flat(ap):
                return ap.rearrange("p a b -> p (a b)")

            one_row = ones.to_broadcast([P, NT // 4 * P])
            dve.tensor_tensor_scan(flat(cmpb), one_row, flat(eq), 0.0, ALU.mult, ALU.add).then_inc(se_v("eqscan"), 1)
            dve.wait_ge(*se_t.at("eqo", b0))
            dve.tensor_copy(base, Tb[:, 0:1]).then_inc(se_v("eqoff"), 1)
            dve.wait_ge(*se_v.at("eqoff", b0))
            dve.tensor_scalar(cmpb, cmpb, base, need, ALU.add, ALU.is_le).then_inc(se_v("eqok"), 1)
            dve.wait_ge(*se_v.at("eqok", b0))
            dve.tensor_tensor(cmpb, cmpb, eq, ALU.mult).then_inc(se_v("eqsel"), 1)
            dve.wait_ge(*se_v.at("eqsel", b0))
            dve.tensor_tensor(gt, gt, cmpb, ALU.add).then_inc(se_v("sel"), 1)
            dve.wait_ge(*se_v.at("sel", b0))
            dve.tensor_tensor_scan(flat(pos), one_row, flat(gt), 0.0, ALU.mult, ALU.add).then_inc(se_v("scan"), 1)
            dve.wait_ge(*se_t.at("selo", b0))
            dve.tensor_copy(base, Tb[:, 0:1]).then_inc(se_v("selbase"), 1)
            dve.wait_ge(*se_v.at("selbase", b0))
            dve.scalar_tensor_tensor(pos, pos, base, gt, ALU.add, ALU.mult).then_inc(se_v("masked"), 1)
            for half in range(2):
                dve.wait_ge(*se_t.at(f"posT{half}", b0))
                dst = posT.rearrange("p (g k) e -> p k g e", g=4)[:, half * 4:half * 4 + 4]
                dve.tensor_copy(dst, Wb[half][:, :].rearrange("p (k g e) -> p k g e", k=4, g=4))\
                    .then_inc(se_v(f"posT{half}"), 1)
            io = iota_e.unsqueeze(1).to_broadcast([P, NT, NE])
            for k in range(2):
                if k:
                    dve.wait_ge(*se_v.at("s0", b0))
                dve.tensor_tensor(ohk, io, e_all[:, :, k:k + 1].to_broadcast([P, NT, NE]), ALU.is_equal)\
                    .then_inc(se_v(f"oh{k}"), 1)
                dve.wait_ge(*se_v.at(f"oh{k}", b0))
                dve.tensor_tensor(ohk, ohk, posT, ALU.mult).then_inc(se_v(f"pr{k}"), 1)
                dve.wait_ge(*se_v.at(f"pr{k}", b0))
                dve.tensor_reduce(slot[:, k, :], ohk, AX.X, ALU.add).then_inc(se_v(f"s{k}"), 1)
            dve.wait_ge(*se_v.at("s1", b0))
            dve.tensor_scalar(shi, slot, float(P), None, ALU.is_gt).then_inc(se_v("hi"), 1)
            dve.wait_ge(*se_v.at("hi", b0))
            dve.scalar_tensor_tensor(slo, shi, -float(P), slot, ALU.mult, ALU.add).then_inc(se_v("lo_"), 1)
            dve.scalar_tensor_tensor(shi, e_all.rearrange("p t k -> p k t"), 2.0, shi, ALU.mult, ALU.add)\
                .then_inc(se_v("hi2"), 1)
            dve.wait_ge(*se_v.at("hi2", b0))
            for i in range(2 * NT // LG):
                k, tiles = i * LG // NT, slice(i * LG % NT, i * LG % NT + LG)
                if i >= 2:
                    dve.wait_ge(*li_t.at(f"m{i - 2}", b0))
                lh, hh = Lh[i % 2], Hh[i % 2]
                dve.tensor_tensor(lh, iota_l.unsqueeze(1).to_broadcast([P, LG, P]),
                                  slo[:, k, tiles].unsqueeze(2).to_broadcast([P, LG, P]), ALU.is_equal)
                dve.tensor_tensor(hh[:, :, 0, :], iota_h.unsqueeze(1).to_broadcast([P, LG, 2 * NE]),
                                  shi[:, k, tiles].unsqueeze(2).to_broadcast([P, LG, 2 * NE]), ALU.is_equal)\
                    .then_inc(li_v(f"oh{i}"), 1)
                dve.wait_ge(*li_v.at(f"oh{i}", b0))
                dve.tensor_tensor(hh[:, :, 1, :], hh[:, :, 0, :],
                                  w_all[:, tiles, k:k + 1].to_broadcast([P, LG, 2 * NE]), ALU.mult).then_inc(li_v(f"w{i}"), 1)
                dve.wait_ge(*li_v.at(f"w{i}", b0))
                dve.tensor_tensor(hh[:, :, 0, :], hh[:, :, 0, :],
                                  tid[:, tiles].unsqueeze(2).to_broadcast([P, LG, 2 * NE]), ALU.mult)\
                    .then_inc(li_v(f"t{i}"), 1)
            dve.wait_ge(*li_t.at(f"m{2 * NT // LG - 1}", b0))
            dve.tensor_copy(tid_l, Tb[:, 0:2 * NE]).then_inc(lf_v("tid"), 1)
            dve.tensor_copy(w_l, Tb[:, 2 * NE:4 * NE]).then_inc(lf_v("w"), 1)
            dve.wait_ge(*lf_v.at("tid", b0))
            dve.tensor_scalar(emp, tid_l, 0.0, None, ALU.is_equal).then_inc(lf_v("empty"), 1)
            dve.wait_ge(*lf_v.at("empty", b0))
            dve.tensor_tensor(emp, emp, iota_s, ALU.mult).then_inc(lf_v("fill"), 1)
            dve.wait_ge(*lf_v.at("fill", b0))
            dve.scalar_tensor_tensor(idx_l, tid_l, -1.0, emp, ALU.add, ALU.add).then_inc(lf_v("idx"), 1)

            def rows_out(e):
                dve.wait_ge(*is_p.at("copy", e - 1))
                w = w_l.rearrange("p (e k) -> p e k", k=2)[:, e.line(1)]
                dve.wait_ge(*yr_t.at("y0", e))
                dve.tensor_scalar(yy[e.slot][:, 0, :], Yb[0][:, :], w[:, 0:1], None, ALU.mult).then_inc(yr_v("y0"), 1)
                dve.wait_ge(*yr_t.at("y1", e))
                dve.tensor_scalar(yy[e.slot][0:CAP2, 1, :], Yb[1][0:CAP2, :], w[0:CAP2, 1:2], None, ALU.mult)\
                    .then_inc(yr_v("y1"), 1)

            def expert(e, first, last):
                for j in range(J + 1):
                    if j == 0:
                        dve.wait_ge(*dn_t.at("d1", e - 1))
                    k = (e.slot * (J + 1) + j) % 2
                    dve.wait_ge(*up_a.at(f"silu{j}", e))
                    u = Ub[k][:, CAP:2 * CAP]
                    if j < J:
                        dve.tensor_tensor(hact[:, j, :], sg[k], u, ALU.mult).then_inc(up_v(f"mul{j}"), 1)
                    else:
                        dve.scalar_tensor_tensor(hact[:, j, :], sg[k], A_SCALE, u, ALU.mult, ALU.mult)\
                            .then_inc(up_v(f"mul{j}"), 1)
                    if j == 1 and not first:
                        rows_out(e - 1)

            run_experts(dve, expert)
            rows_out(Batch(0, NE - 1))

            for i in range(NB + 1):
                if i < NB:
                    b, p = Batch(0, i), i % 2
                    dve.wait_ge(*fi_v.at("out", b - 2))
                    dve.wait_ge(ld_f[i], 16)
                    for tb in range(TB):
                        m = dve.bn_stats(ln_st[p][:, tb, :], fin[i][:, tb, :])
                    m.then_inc(fb_v("bn"), 1)
                    dve.wait_ge(*fb_v.at("bn", b))
                    for tb in range(TB):
                        m = dve.bn_aggr(ln_mv[p][:, tb, :], ln_st[p][:, tb, :])
                    m.then_inc(fb_v("aggr"), 1)
                if i:
                    b, p = Batch(0, i - 1), (i - 1) % 2
                    dve.wait_ge(*fi_p.at("rstd", b))
                    for tb in range(TB):
                        m = dve.tensor_scalar(fin[i - 1][:, tb, :], fin[i - 1][:, tb, :], ln_mv[p][:, tb, 0:1],
                                              ln_rs[p][:, tb:tb + 1], ALU.subtract, ALU.mult)
                    m.then_inc(fi_v("out"), 1)

        @block.gpsimd
        def _(pool):
            start(pool, "pool")
            def select(ap, pattern, base_, mult, op, fill, done):
                pool.affine_select(out=ap, in_=ap, pattern=pattern, compare_op=op, fill=fill, base=base_,
                                   channel_multiplier=mult).then_inc(done, 1)

            pool.memset(ident, 0.0).then_inc(cs_p("ident0"), 1)
            pool.wait_ge(*cs_p.at("ident0", b0))
            select(ident, [[-1, P]], 0, 1, ALU.not_equal, 1.0, cs_p("ident"))
            pool.memset(sel, 0.0).then_inc(cs_p("sel0"), 1)
            for q in range(3):
                pool.wait_ge(*cs_p.at(f"sel{q}", b0))
                select(sel, [[-1, NH], [0, P]], -32 * q, 1, ALU.not_equal, 1.0, cs_p(f"sel{q + 1}"))
            pool.iota(iota_e, pattern=[[1, NE]], base=0, channel_multiplier=0,
                      allow_small_or_imprecise_dtypes=True).then_inc(cs_p("iota"), 1)
            for t in kz:
                m = pool.memset(t, 0.0)
            m.then_inc(cs_p("kz"), 1)
            pool.wait_ge(*cs_v.at("misc", b0))

            def power(var, rs, eps, done_eps, wait_eps, done):
                hold(pool)
                pool.tensor_scalar(rs, var, eps, None, ALU.add).then_inc(done_eps, 1)
                pool.wait_ge(*wait_eps)
                pool.tensor_tensor(rs, rs, negh, ALU.pow).then_inc(done, 1)

            def mask(b, h):
                pool.wait_ge(*at_a.at(f"exp{h}", b))
                hold(pool)
                d = Dm[h % ND][:, 0:TB * P].rearrange("p (a s) -> p a s", a=TB)
                m = pool.affine_select(out=d, in_=d, pattern=[[0, TB], [1, P]], compare_op=ALU.is_ge, fill=0.0, base=0,
                                       channel_multiplier=-1)
                m.then_inc(at_p(f"mask{h}"), 1)

            def step(n, a, s, r, x1, x2):
                for h in range(NH):
                    if r and h == 0:
                        pool.wait_ge(*l2_v.at("aggr2", n - 2))
                        power(mv2[:, :, 1], rs2, LN_EPS, l2_p("eps2"), l2_p.at("eps2", n - 2), l2_p("rstd2"))
                    if r and h == 1:
                        pool.wait_ge(*l2_v.at("aggr3", n - 2))
                        power(mv3[:, :, 1], rs3, LN_EPS, l2_p("eps3"), l2_p.at("eps3", n - 2), l2_p("rstd3"))
                    if a and h == 3:
                        pool.wait_ge(*n1_v.at("aggr", n))
                        power(mv1[:, :, 1], rs1, LN_EPS, n1_p("eps"), n1_p.at("eps", n), n1_p("rstd"))
                    if r and h == 3:
                        pool.wait_ge(*ro_v.at("vars", n - 2))
                        pool.tensor_tensor(vr[:, 0, :], vr[:, 0, :], posh, ALU.pow).then_inc(ro_p("std"), 1)
                        pool.tensor_tensor(vr[:, 1, :], vr[:, 1, :], posh, ALU.pow).then_inc(ro_p("l2"), 1)
                    if s and h + 2 < NH:
                        mask(n - 1, h + 2)
                if a:
                    mask(n, 0)
                    mask(n, 1)

            run_pipeline(pool, step)

            pool.wait_ge(*ro_v.at("save", bl))
            pool.wait_ge(*ro_t.at("lg", bl))
            for done in st_x2 + st_acc:
                pool.wait_ge(done, 16 * NB // 2 + 16)
            pool.memset(blk, 0.0)
            pool.memset(low, 0.0).then_inc(se_p("blk0"), 1)
            for i, d in enumerate((0, -1, 1, -2, 2, -3, 3)):
                pool.wait_ge(*se_p.at(f"blk{i}", b0))
                if d < 0:
                    select(low, [[-1, P]], -32 * d, 1, ALU.not_equal, 1.0, se_p(f"low{-d}"))
                select(blk, [[-1, P]], -32 * d, 1, ALU.not_equal, 1.0, se_p(f"blk{i + 1}"))
            pool.iota(iota_l, pattern=[[1, P]], base=1, channel_multiplier=0, allow_small_or_imprecise_dtypes=True)
            pool.iota(iota_h, pattern=[[1, 2 * NE]], base=0, channel_multiplier=0, allow_small_or_imprecise_dtypes=True)
            pool.iota(tid, pattern=[[P, NT]], base=1, channel_multiplier=1, allow_small_or_imprecise_dtypes=True)
            pool.iota(iota_s.rearrange("p (e k) -> p e k", k=2), pattern=[[0, NE], [P, 2]], base=NTOK + 1,
                      channel_multiplier=1, allow_small_or_imprecise_dtypes=True).then_inc(se_p("iotas"), 1)

            def columns(e, ix, done):
                pool.tensor_copy(ix[e.slot], idx_l.rearrange("p (e k) -> p e k", k=2)[:, e.line(1)]).then_inc(done, 1)

            def gather(e):
                pool.wait_ge(*xr_t.at("x1", e - 2))
                columns(e, idx_g, ig_p("copy"))
                pool.wait_ge(*ig_p.at("copy", e))
                hold(pool)
                for k, n in enumerate((P, CAP2)):
                    pool.indirect_dma_start(out=xg[e.slot][0:n, k, :], out_offset=None, in_=x2_d,
                                            in_offset=bass.IndirectOffsetOnAxis(ap=idx_g[e.slot][0:n, k:k + 1], axis=0))\
                        .then_inc(ld_g[e.slot], 16)

            def scatter(e):
                if e.off:
                    pool.wait_ge(st_y, e.line(32))
                columns(e, idx_s, is_p("copy"))
                pool.wait_ge(*is_p.at("copy", e))
                pool.wait_ge(*yr_v.at("y1", e))
                hold(pool)
                for k, n in enumerate((P, CAP2)):
                    pool.indirect_dma_start(out=acc_d,
                                            out_offset=bass.IndirectOffsetOnAxis(ap=idx_s[e.slot][0:n, k:k + 1], axis=0),
                                            in_=yy[e.slot][0:n, k, :], in_offset=None, compute_op=ALU.add)\
                        .then_inc(st_y, 16)

            pool.wait_ge(*lf_v.at("idx", b0))
            pool.wait_ge(st_dum, 64)
            gather(b0)
            gather(b0 + 1)
            for p in range(2):
                scatter(Batch(0, p))
                gather(Batch(0, 2 + p))
            with pool.Fori(0, (NE - 4) // 2) as i:
                t = i * 2
                for p in range(2):
                    scatter(Batch(t, 2 + p))
                    gather(Batch(t, 4 + p))
            for p in range(2):
                scatter(Batch(0, NE - 2 + p))

            for i in range(NB):
                b, p = Batch(0, i), i % 2
                pool.wait_ge(*fb_v.at("aggr", b))
                pool.wait_ge(*fi_v.at("out", b - 2))
                power(ln_mv[p][:, :, 1], ln_rs[p], LN_EPS, fi_p("eps"), fi_p.at("eps", b), fi_p("rstd"))


def kernel(**inputs):
    import numpy as np
    import concourse.bacc as bacc
    from concourse.bass_utils import run_bass_kernel_spmd

    g = {k.replace("L0_", ""): np.asarray(v) for k, v in inputs.items()}

    def chunks(a):
        a = a.reshape(a.shape[:-2] + (a.shape[-2] // P, P, a.shape[-1]))
        return np.swapaxes(a, -3, -2)

    def column(a):
        return a.reshape(-1, P).T

    arrays = {
        "xT": chunks(np.swapaxes(g["x"], 1, 2)),
        "kT": chunks(np.swapaxes(g["ctx_1024"], 1, 2)),
        "v": np.swapaxes(g["ctx_1024"].reshape(NB, TB, P, NH, DH), 1, 2),
        "decay": column(g["attn_decay_logit"]),
        "WT": chunks(g["attn_W"].T),
        "b": column(g["attn_b"]),
        "cw": np.swapaxes(g["attn_conv_w"].reshape(C, P, TAPS), 0, 1),
        "cb": column(g["attn_conv_b"]),
        "wi": chunks(g["xattn_igate_w"].T),
        "wf": chunks(g["xattn_fgate_w"].T),
        "ib": g["xattn_igate_b"][:, None],
        "fb": g["xattn_fgate_b"][:, None],
        "ln": g["xattn_ln_scale"][None],
        "r1x": chunks(g["ffn_r1_w"][:, :D].T),
        "r1s": g["ffn_r1_w"][:, D:].T,
        "r1b": column(g["ffn_r1_b"]),
        "r2": chunks(g["ffn_r2_w"].T),
        "wup": chunks(np.swapaxes(g["ffn_w_up"], 1, 2)),
        "wdn": chunks(np.swapaxes(g["ffn_w_down"], 1, 2)),
        "aup": chunks(np.swapaxes(g["ffn_a_up"], 1, 2)),
        "adn": np.swapaxes(g["ffn_a_down"], 1, 2),
    }
    nc = bacc.Bacc("TRN2", target_bir_lowering=False, num_devices=1)
    args, feed = [], {}
    for name, a in arrays.items():
        a = np.ascontiguousarray(a)
        feed[f"in_{name}"] = a
        args.append(nc.dram_tensor(f"in_{name}", a.shape, mybir.dt.from_np(a.dtype), kind="ExternalInput").ap())
    out = nc.dram_tensor("out", (NB, T, D), F32, kind="ExternalOutput")
    decoder_kernel(nc, *args, out.ap())
    r = run_bass_kernel_spmd(nc, [feed], core_ids=[0])
    return r.results[0]["out"]
```
